# Optimizing a Trainium2 kernel written in Bass

```python
import numpy as np
import jax
import jax.numpy as jnp

def _softmax(x, axis=-1):
    return jax.nn.softmax(x, axis=axis)
def _gelu(x):
    return jax.nn.gelu(x, approximate=True)
def _silu(x):
    return jax.nn.silu(x)
def _sigmoid(x):
    return jax.nn.sigmoid(x)
def _layernorm(x, axis=-1, eps=1e-5):
    m = jnp.mean(x, axis=axis, keepdims=True)
    v = jnp.var(x, axis=axis, keepdims=True)
    return (x - m) / jnp.sqrt(v + eps)
def _scatter_add(tgt, idx, src, axis=0):
    return tgt.at[idx].add(src)
def _segment_sum(src, seg, n):
    return jax.ops.segment_sum(src, seg, n)

kernel_name = 'mk_conv_preact_d1_conv_nchw256_61aab5'

def setup_inputs(seed: int = 0):
    np.random.seed(seed)
    _w = jnp.asarray
    def _rec_inputs():
        import jax
        import jax.numpy as jnp
        _gk = jax.random.key(seed)
        x = -0.0002928 + 1 * jax.random.normal(jax.random.fold_in(_gk, 1), (4, 256, 64, 64), jnp.float32)
        return x
    x = _rec_inputs()
    def _L0_conv_setup():
        import jax, jax.numpy as jnp
        import numpy as np
        B, C, H, W = (4, 256, 64, 64)
        CQ = C // 4
        key = jax.random.key(seed)
        k1, k2, k3, k4, k5 = jax.random.split(key, 5)
        x = jax.random.normal(k1, (B, C, H, W), dtype=jnp.float32)
        Wq = jax.random.normal(k2, (CQ, C), dtype=jnp.float32) * (1.0 / np.sqrt(C))
        Wk = jax.random.normal(k3, (CQ, C), dtype=jnp.float32) * (1.0 / np.sqrt(C))
        Wv = jax.random.normal(k4, (C, C), dtype=jnp.float32) * (1.0 / np.sqrt(C))
        gamma = jax.random.normal(k5, (1,), dtype=jnp.float32)
        return {'x': x, 'Wq': Wq, 'Wk': Wk, 'Wv': Wv, 'gamma': gamma}
    _L0_conv_all = _L0_conv_setup()
    _L0_conv_in = {k: v for k, v in _L0_conv_all.items() if k in ('Wq', 'Wk', 'Wv', 'gamma', )}
    del _L0_conv_all

    return {
        "x": x,
        "L0_conv_Wq": _L0_conv_in["Wq"],
        "L0_conv_Wk": _L0_conv_in["Wk"],
        "L0_conv_Wv": _L0_conv_in["Wv"],
        "L0_conv_gamma": _L0_conv_in["gamma"],
    }

def reference(x, L0_conv_Wq, L0_conv_Wk, L0_conv_Wv, L0_conv_gamma):
    import jax
    import jax.numpy as jnp
    def _L0_conv_ref(x, Wq, Wk, Wv, gamma):
        import jax, jax.numpy as jnp
        import numpy as np
        B, C, H, W = (4, 256, 64, 64)
        CQ = C // 4
        size = x.shape
        xf = x.reshape(size[0], size[1], -1)
        f = jnp.einsum('qc,bcn->bqn', Wq, xf)
        g = jnp.einsum('qc,bcn->bqn', Wk, xf)
        h = jnp.einsum('vc,bcn->bvn', Wv, xf)
        scores = jnp.einsum('bqn,bqm->bnm', f, g)
        beta = jax.nn.softmax(scores, axis=1)
        o = jnp.einsum('bvn,bnm->bvm', h, beta)
        out = gamma[0] * o + xf
        return out.reshape(size)

    def _gn(v, G=32, eps=1e-5):
        B_, C_, H_, W_ = v.shape
        g = v.reshape(B_, G, C_ // G, H_, W_)
        m = jnp.mean(g, axis=(2, 3, 4), keepdims=True)
        s = jnp.var(g, axis=(2, 3, 4), keepdims=True)
        return ((g - m) / jnp.sqrt(s + eps)).reshape(v.shape)

    def _ln_c(v, eps=1e-6):
        m = jnp.mean(v, axis=1, keepdims=True)
        s = jnp.var(v, axis=1, keepdims=True)
        return (v - m) / jnp.sqrt(s + eps)

    def _ln_t(v, eps=1e-5):
        m = jnp.mean(v, axis=-1, keepdims=True)
        s = jnp.var(v, axis=-1, keepdims=True)
        return (v - m) / jnp.sqrt(s + eps)

    def _to_tokens(v):
        B_, C_, H_, W_ = v.shape
        return v.reshape(B_, C_, H_ * W_).transpose(0, 2, 1)
    def _from_tokens(t, like):
        B_, C_, H_, W_ = like.shape
        return t.transpose(0, 2, 1).reshape(B_, C_, H_, W_)

    x = x + _L0_conv_ref(_gn(x), L0_conv_Wq, L0_conv_Wk, L0_conv_Wv, L0_conv_gamma)
    return x


_drawn_inputs = setup_inputs


def setup_inputs(seed=0):
    import zlib

    import numpy as np

    out = dict(_drawn_inputs(seed))
    spreads = {}
    factors = {}
    for name, (base, spread) in spreads.items():
        noise = np.random.default_rng([zlib.crc32(name.encode()), seed]).standard_normal(out[name].shape)
        drawn = base * np.exp(spread * noise) if base else spread * noise
        out[name] = jnp.asarray(drawn.astype(out[name].dtype))
    for name, factor in factors.items():
        out[name] = (out[name] * factor).astype(out[name].dtype)
    return out
```

```python
import concourse.bass as bass
from concourse import mybir
from contextlib import ExitStack


def groupnorm_attention(nc, x, wqT, wkT, wvT, gamma, out):
    f32, f16, i32 = mybir.dt.float32, mybir.dt.float16, mybir.dt.int32
    ALU, ACT, AX = mybir.AluOpType, mybir.ActivationFunctionType, mybir.AxisListType

    BATCH, C, N = x.shape
    P = 128
    H = C // P
    CQ = wqT.shape[1]
    CH = 512
    NCH = N // CH
    T = N // P
    MT = CH // P
    GRP = 4
    RING = 2 * GRP
    VW = C + 2 + C
    VL0 = C + 2
    GN = 8
    NG = 32 // GN
    PROJ = NCH + T
    EPS = 1e-5
    SHIFT = 8.0
    ROWM = 64.0
    RSQRT_GUESS = 0x5F3759DF
    COEF = 22
    assert 2 * CQ == P and C == H * P and T == 32 and NCH == 8

    xv = x.rearrange("b (h p) n -> b p h n", p=P)
    ov = out.rearrange("b (h p) n -> b p h n", p=P)

    with ExitStack() as ctx:
        def sb(name, shape, dt):
            return ctx.enter_context(nc.sbuf_tensor(name, shape, dt))

        def sem(name):
            return ctx.enter_context(nc.semaphore(name))

        F1 = sb("F1", [P, N], f16)
        F2 = sb("F2", [P, N], f16)
        G1 = sb("G1", [P, N], f16)
        G2 = sb("G2", [P, N], f16)
        FL = sb("FL", [CQ, N], f16)
        V = sb("V", [P, T * VW], f16)
        XH = sb("XH", [P, H, N], f16)
        XL = sb("XL", [P, H, N], f16)
        wqk = sb("wqk", [P, H, P], f32)
        wv = sb("wv", [P, H, C], f32)
        wqkh = sb("wqkh", [P, H, P], f16)
        wqkl = sb("wqkl", [P, H, P], f16)
        wvh = sb("wvh", [P, H, C], f16)
        wvl = sb("wvl", [P, H, C], f16)
        gam = sb("gam", [P, 1], f32)
        ident = sb("ident", [P, P], f32)
        ident16 = sb("ident16", [P, P], f16)
        PF = sb("PF", [P, RING, CH], f32)
        PH = sb("PH", [P, RING, CH], f16)
        PL = sb("PL", [P, RING, CH], f16)
        OSB = sb("OSB", [P, MT, C], f32)
        RES = sb("RES", [P, H, CH], f32)
        x0 = sb("x0", [P, H, N], f32)
        xin_norm = sb("xin_norm", [P, H, CH], f32)
        xin_stat = sb("xin_stat", [P, H, CH], f32)
        xin_res = sb("xin_res", [P, H, CH], f32)
        XNF = sb("XNF", [P, H, CH], f32)
        mx = sb("mx", [P, MT, NCH], f32)
        mxc = sb("mxc", [P, MT], f32)
        mpair = sb("mpair", [P, MT, 2], f16)
        rden = sb("rden", [P, MT], f32)
        stats = sb("stats", [P, H, NCH, 6], f32)
        mv = sb("mv", [P, H, 2], f32)
        cm = sb("cm", [P, 32], f32)
        cv = sb("cv", [P, 32], f32)
        tm = sb("tm", [P, NG, GN], f32)
        tv = sb("tv", [P, NG, GN], f32)
        gmean = sb("gmean", [P, NG], f32)
        gvar = sb("gvar", [P, NG], f32)
        gr = sb("gr", [P, NG], f32)
        gt = sb("gt", [P, NG], f32)
        bm = sb("bm", [P, NG, GN], f32)
        br = sb("br", [P, NG, GN], f32)
        nmean = sb("nmean", [P, 32], f32)
        nrstd = sb("nrstd", [P, 32], f32)
        rscale = sb("rscale", [P, H], f32)
        rbias = sb("rbias", [P, H], f32)

        O = ctx.enter_context(nc.psum_tensor("O", [P, MT, 512], f32))
        S = ctx.enter_context(nc.psum_tensor("S", [P, 2, 512], f32))
        ST = ctx.enter_context(nc.psum_tensor("ST", [P, 2, 512], f32))

        w_in = sem("w_in")
        x0_in = [sem(f"x0_in{i}") for i in range(4)]
        x1_in = sem("x1_in")
        norm_in = sem("norm_in")
        stat_in = sem("stat_in")
        res_in = sem("res_in")
        fg_moved = [sem("fg_moved0"), sem("fg_moved1")]
        out_stored = sem("out_stored")
        consts = sem("consts")
        w_split = sem("w_split")
        w_hi = sem("w_hi")
        x1_stats = sem("x1_stats")
        stats_done = sem("stats_done")
        coef_step = sem("coef_step")
        coefs_ready = sem("coefs_ready")
        xn_ready = sem("xn_ready")
        xh_ready = sem("xh_ready")
        xl_ready = sem("xl_ready")
        proj_ready = sem("proj_ready")
        proj_hi = sem("proj_hi")
        proj_bank_free = sem("proj_bank_free")
        st_ready = sem("st_ready")
        st_bank_free = sem("st_bank_free")
        max_step = sem("max_step")
        mpair_ready = sem("mpair_ready")
        mrow_psum = sem("mrow_psum")
        mrow_ready = sem("mrow_ready")
        s_ready = sem("s_ready")
        exp_done = sem("exp_done")
        pl_ready = sem("pl_ready")
        o_ready = sem("o_ready")
        rden_ready = sem("rden_ready")
        osb_ready = sem("osb_ready")
        ot_ready = sem("ot_ready")
        res_ready = sem("res_ready")
        out_ready = sem("out_ready")

        block = ctx.enter_context(nc.Block())
        ds = bass.ds

        @block.sync
        def _(sp):
            for q in range(4):
                sp.dma_start(x0[:, :, q * N // 4:(q + 1) * N // 4],
                             xv[0, :, :, q * N // 4:(q + 1) * N // 4]).then_inc(x0_in[q], 16)
            sp.dma_start(wqk[:, :, 0:CQ], wqT.rearrange("(h p) q -> p h q", p=P)).then_inc(w_in, 16)
            sp.dma_start(wqk[:, :, CQ:P], wkT.rearrange("(h p) q -> p h q", p=P)).then_inc(w_in, 16)
            sp.dma_start(wv[:, :, :], wvT.rearrange("(h p) v -> p h v", p=P)).then_inc(w_in, 16)
            sp.dma_start(gam[:, :], gamma).then_inc(w_in, 16)
            x1 = PF[:, :, :].rearrange("p r n -> p (r n)").rearrange("p (h n) -> p h n", h=H)
            for half in range(2):
                if half:
                    sp.wait_ge(x1_stats, 1)
                sp.dma_start(x1, xv[1, :, :, half * N // 2:(half + 1) * N // 2]).then_inc(x1_in, 16)
            with sp.Fori(0, BATCH) as b:
                for half in range(2):
                    sp.wait_ge(proj_bank_free, b * PROJ + 4 + 4 * (half + 1))
                    cols = slice(half * N // 2, (half + 1) * N // 2)
                    sp.dma_start(F1[CQ:P, cols], FL[:, cols]).then_inc(fg_moved[half], 16)
                    sp.dma_start(F2[CQ:P, cols], F1[0:CQ, cols]).then_inc(fg_moved[half], 16)
                    sp.dma_start(G1[0:CQ, cols], G1[CQ:P, cols]).then_inc(fg_moved[half], 16)
                with sp.Fori(0, NCH) as j:
                    c = b * NCH + j
                    col = ds(j * CH, CH)
                    sp.wait_ge(res_ready, 2 * c + 1)
                    sp.dma_start(xin_res[:, :, :], xv[b, :, :, col]).then_inc(res_in, 16)
                    sp.wait_ge(xn_ready, c + NCH)
                    sp.dma_start(xin_norm[:, :, :], xv[(b + 1) % BATCH, :, :, col]).then_inc(norm_in, 16)
                    sp.wait_ge(stats_done, c + 1)
                    sp.dma_start(xin_stat[:, :, :], xv[(b + 2) % BATCH, :, :, col]).then_inc(stat_in, 16)
                    sp.wait_ge(out_ready, 2 * c + 3)
                    sp.dma_start(ov[b, :, :, col], RES[:, :, :]).then_inc(out_stored, 16)
            sp.wait_ge(out_stored, 16 * BATCH * NCH + 1)

        @block.gpsimd
        def _(pool):
            pool.memset(F2[0:CQ, :], 0.0).then_inc(consts, 1)
            pool.memset(G2[0:CQ, :], 0.0).then_inc(consts, 1)
            pool.memset(V[:, :].rearrange("p (t w) -> p t w", w=VW)[:, :, C:C + 1], 1.0).then_inc(consts, 1)
            pool.memset(ident[:, :], 0.0).then_inc(consts, 1)
            pool.memset(ident16[:, :], 0.0).then_inc(consts, 1)
            pool.wait_ge(consts, 5)
            pool.memset(F2[0:2, :], 1.0).then_inc(consts, 1)
            pool.wait_ge(consts, 6)
            pool.memset(F2[0:1, :], ROWM).then_inc(consts, 1)
            for m in (ident, ident16):
                pool.affine_select(out=m[:, :], in_=m[:, :], compare_op=ALU.not_equal, fill=1.0,
                                   base=0, pattern=[[-1, P]], channel_multiplier=1).then_inc(consts, 1)

        @block.tensor
        def _(pe):
            mm = nc.tensor.matmul

            def transposed_scores(j, i, q, sigma, bank):
                pe.wait_ge(st_bank_free, sigma + 1)
                mm(ST[:, bank, :], G1[:, ds(j * CH + i * P, P)], F1[:, ds(q * CH, CH)],
                   start=True, stop=True).then_inc(st_ready, 1)

            def scores(j, t, bank):
                mm(S[:, bank, :], F1[:, ds(t * P, P)], G1[:, ds(j * CH, CH)], start=True, stop=False)
                mm(S[:, bank, :], F2[:, ds(t * P, P)], G2[:, ds(j * CH, CH)],
                   start=False, stop=True).then_inc(s_ready, 1)

            def weigh(t, slot, i, first=False, last=False):
                ph = PH[:, slot, i * P:(i + 1) * P]
                mm(O[:, i, 0:C + 1], ph, V[:, ds(t * VW, C + 1)], start=first, stop=False)
                mm(O[:, i, 0:C], ph, V[:, ds(t * VW + VL0, C)], start=False, stop=False)
                return mm(O[:, i, 0:C + 1], PL[:, slot, i * P:(i + 1) * P], V[:, ds(t * VW, C + 1)],
                          start=False, stop=last)

            def maxima_to_rows(c):
                pe.wait_ge(mpair_ready, c + 1)
                for i in range(MT):
                    m = mm(ST[0:2, 0, i * P:(i + 1) * P], mpair[:, i, :], ident16[:, :], start=True, stop=True)
                m.then_inc(mrow_psum, 1)

            def group(j, c, g, half, first=False, st=0):
                for k in range(GRP):
                    t = GRP * g + k
                    tau = c * T + t
                    pe.wait_ge(exp_done, tau + GRP - 1)
                    scores(j, t + GRP, k % 2)
                    pe.wait_ge(pl_ready, tau + 1)
                    for i in range(MT):
                        weigh(t, half * GRP + k, i, first=first and k == 0)
                        if st == 2 and i % 2:
                            w = 2 * k + i // 2
                            transposed_scores(j + 1, w % MT, 2 * g + w // MT,
                                              (c + 1) * T + 2 * t + i // 2, i // 2)
                        if st == 1 and i == 1:
                            transposed_scores(j + 1, k, g + 2, (c + 1) * T + RING + t, k % 2)

            def chunk(b, j, more):
                c = b * NCH + j
                pe.wait_ge(out_ready, 2 * c + 1)
                group(j, c, 0, 0, first=True, st=2 * more)
                group(j, c, 1, 1, st=2 * more)
                with pe.Fori(1, T // RING - 1) as p:
                    group(j, c, 2 * p, 0, st=1 * more)
                    group(j, c, 2 * p + 1, 1, st=1 * more)
                for k in range(GRP):
                    t = T - RING + k
                    if more and k == 2:
                        maxima_to_rows(c + 1)
                    pe.wait_ge(exp_done, c * T + t + GRP - 1)
                    scores(j, t + GRP, k % 2)
                    pe.wait_ge(pl_ready, c * T + t + 1)
                    for i in range(MT):
                        weigh(t, k, i)
                if more:
                    pe.wait_ge(mrow_ready, c + 2)
                for i in range(MT):
                    if more:
                        pe.wait_ge(exp_done, c * T + T + i - 1)
                        scores(j + 1, i, i % 2)
                    for k in range(GRP):
                        t = T - GRP + k
                        if i == 0:
                            pe.wait_ge(pl_ready, c * T + t + 1)
                        w = weigh(t, GRP + k, i, last=k == GRP - 1)
                    w.then_inc(o_ready, 1)
                for i in range(MT):
                    pe.wait_ge(osb_ready, c * MT + i + 1)
                    for h in range(H):
                        m = nc.tensor.transpose(ST[:, h, i * P:(i + 1) * P], OSB[:, i, h * P:(h + 1) * P],
                                                ident[:, :])
                m.then_inc(ot_ready, 1)

            pe.wait_ge(consts, 9)
            pe.wait_ge(w_split, 2)
            with pe.Fori(0, BATCH) as b:
                with pe.Fori(0, NCH // MT) as r:
                    for k in range(MT):
                        i = MT * r + k
                        n = ds(i * CH, CH)
                        pe.wait_ge(xl_ready, b * NCH + i + 2)
                        pe.wait_ge(proj_bank_free, b * PROJ + i + 1)
                        for h in range(H):
                            mm(O[:, k, :], wqkh[:, h, :], XH[:, h, n], start=h == 0, stop=False)
                            mm(O[:, k, :], wqkl[:, h, :], XH[:, h, n], start=False, stop=False)
                            m = mm(O[:, k, :], wqkh[:, h, :], XL[:, h, n], start=False, stop=h == H - 1)
                        m.then_inc(proj_ready, 1)
                for half in range(2):
                    with pe.Fori(half * NCH // 2, (half + 1) * NCH // 2) as r:
                        for k in range(MT):
                            i = MT * r + k
                            n = ds(i * P, P)
                            pe.wait_ge(proj_bank_free, b * PROJ + NCH + i + 1)
                            for h in range(H):
                                mm(O[:, k, 0:C], XH[:, h, n], wvh[:, h, :], start=h == 0, stop=False)
                                mm(O[:, k, 0:C], XH[:, h, n], wvl[:, h, :], start=False, stop=False)
                                m = mm(O[:, k, 0:C], XL[:, h, n], wvh[:, h, :], start=False, stop=h == H - 1)
                            m.then_inc(proj_ready, 1)
                            if k == 0:
                                pe.wait_ge(out_ready, 2 * NCH * b + 1)
                                pe.wait_ge(fg_moved[half], 48 * (b + 1))
                            transposed_scores(0, k, r, b * NCH * T + i, k % 2)
                maxima_to_rows(b * NCH)
                pe.wait_ge(mrow_ready, b * NCH + 1)
                for k in range(GRP):
                    if k >= 2:
                        pe.wait_ge(exp_done, b * NCH * T + k - 1)
                    scores(0, k, k % 2)
                with pe.Fori(0, NCH - 1) as j:
                    chunk(b, j, True)
                chunk(b, NCH - 1, False)

        @block.scalar
        def _(act):
            def exps(c, g, half, k):
                act.wait_ge(s_ready, c * T + GRP * g + k + 1)
                slot = half * GRP + k
                nc.scalar.activation(PH[:, slot, :], S[:, k % 2, :], ACT.Exp, bias=SHIFT)
                nc.scalar.activation(PF[:, slot, :], S[:, k % 2, :], ACT.Exp, bias=SHIFT).then_inc(exp_done, 1)

            def chunk(b, j, more):
                c = b * NCH + j
                for k in range(GRP):
                    exps(c, 1, 1, k)
                with act.Fori(1, T // RING - 1) as p:
                    for k in range(GRP):
                        exps(c, 2 * p, 0, k)
                    for k in range(GRP):
                        exps(c, 2 * p + 1, 1, k)
                for k in range(GRP):
                    exps(c, NCH - 2, 0, k)
                for k in range(GRP):
                    exps(c, NCH - 1, 1, k)
                    if k == 1:
                        act.wait_ge(coefs_ready, b + 2)
                        act.wait_ge(res_in, 16 * (c + 1))
                        act.wait_ge(out_stored, 16 * c + 1)
                        for h in range(H):
                            nc.scalar.activation(RES[:, h, :], xin_res[:, h, :], ACT.Identity,
                                                 scale=rscale[:, h:h + 1], bias=rbias[:, h:h + 1]).then_inc(res_ready, 1)
                    if k == 2:
                        round_piece(j, NCH + c)
                if more:
                    act.wait_ge(mrow_psum, c + 2)
                    nc.scalar.copy(G2[0:2, ds((j + 1) * CH, CH)], ST[0:2, 0, :]).then_inc(mrow_ready, 1)
                    for k in range(GRP):
                        exps(c + 1, 0, 0, k)

            def round_piece(j, n):
                act.wait_ge(xn_ready, n + 1)
                nc.scalar.copy(XH[:, :, ds(j * CH, CH)], XNF[:, :, :]).then_inc(xh_ready, 1)

            act.wait_ge(w_in, 64)
            nc.scalar.copy(wqkh[:, :, :], wqk[:, :, :])
            nc.scalar.copy(wvh[:, :, :], wv[:, :, :]).then_inc(w_hi, 1)
            with act.Fori(0, NCH) as j:
                round_piece(j, j)
            act.wait_ge(coefs_ready, 1)
            with act.Fori(0, BATCH) as b:
                with act.Fori(0, NCH // MT) as r:
                    for k in range(MT):
                        i = MT * r + k
                        n = ds(i * CH, CH)
                        act.wait_ge(proj_ready, b * PROJ + i + 1)
                        nc.scalar.copy(F1[0:CQ, n], O[0:CQ, k, :])
                        nc.scalar.copy(G1[CQ:P, n], O[CQ:P, k, :]).then_inc(proj_hi, 1)
                with act.Fori(0, T // MT) as r:
                    for k in range(MT):
                        i = MT * r + k
                        act.wait_ge(proj_ready, b * PROJ + NCH + i + 1)
                        nc.scalar.copy(V[:, ds(i * VW, C)], O[:, k, 0:C]).then_inc(proj_hi, 1)
                act.wait_ge(mrow_psum, b * NCH + 1)
                nc.scalar.copy(G2[0:2, 0:CH], ST[0:2, 0, :]).then_inc(mrow_ready, 1)
                for k in range(GRP):
                    exps(b * NCH, 0, 0, k)
                with act.Fori(0, NCH - 1) as j:
                    chunk(b, j, True)
                chunk(b, NCH - 1, False)

        @block.vector
        def _(dve):
            ve = nc.vector

            def coefficients(n):
                base = n * COEF
                done = [0]

                def step(ins):
                    done[0] += 1
                    ins.then_inc(coef_step, 1)
                    dve.wait_ge(coef_step, base + done[0])

                for h in range(H):
                    last = ve.bn_aggr(mv[:, h, :], stats[:, h, :, :].rearrange("p a b -> p (a b)"))
                step(last)
                ve.tensor_copy(cm[:, 0:H], mv[:, :, 0])
                step(ve.tensor_copy(cv[:, 0:H], mv[:, :, 1]))
                flat = "p a b -> p (a b)"
                ve.transpose(tm[:, :, :].rearrange(flat), cm[:, :])
                step(ve.transpose(tv[:, :, :].rearrange(flat), cv[:, :]))
                step(ve.tensor_reduce(gmean[:, :], tm[:, :, :], axis=AX.X, op=ALU.add))
                step(ve.tensor_scalar(gmean[:, :], gmean[:, :], 1.0 / GN, None, ALU.mult))
                spread = gmean[:, :].unsqueeze(2).to_broadcast([P, NG, GN])
                ve.tensor_copy(bm[:, :, :], spread)
                step(ve.tensor_tensor(tm[:, :, :], tm[:, :, :], spread, ALU.subtract))
                step(ve.tensor_tensor(tm[:, :, :], tm[:, :, :], tm[:, :, :], ALU.mult))
                step(ve.tensor_tensor(tv[:, :, :], tv[:, :, :], tm[:, :, :], ALU.add))
                step(ve.tensor_reduce(gvar[:, :], tv[:, :, :], axis=AX.X, op=ALU.add))
                step(ve.tensor_scalar(gvar[:, :], gvar[:, :], 1.0 / GN, EPS, ALU.mult, ALU.add))
                step(ve.tensor_scalar(gt[:, :].bitcast(i32), gvar[:, :].bitcast(i32), 1, None,
                                      ALU.logical_shift_right))
                step(ve.tensor_scalar(gr[:, :].bitcast(i32), gt[:, :].bitcast(i32), -1.0, float(RSQRT_GUESS),
                                      ALU.mult, ALU.add))
                for _ in range(3):
                    step(ve.scalar_tensor_tensor(gt[:, :], gr[:, :], -0.5, gr[:, :], ALU.mult, ALU.mult))
                    step(ve.tensor_tensor(gt[:, :], gt[:, :], gvar[:, :], ALU.mult))
                    step(ve.scalar_tensor_tensor(gr[:, :], gt[:, :], 1.5, gr[:, :], ALU.add, ALU.mult))
                ve.transpose(nmean[:, :], bm[:, :, :].rearrange(flat))
                step(ve.tensor_copy(br[:, :, :], gr[:, :].unsqueeze(2).to_broadcast([P, NG, GN])))
                assert done[0] == COEF
                ve.transpose(nrstd[:, :], br[:, :, :].rearrange(flat)).then_inc(coefs_ready, 1)

            def normalise_piece(src, n):
                dve.wait_ge(xl_ready, n + 1)
                for h in range(H):
                    last = ve.tensor_scalar(XNF[:, h, :], src(h), nmean[:, h:h + 1], nrstd[:, h:h + 1],
                                            ALU.subtract, ALU.mult)
                last.then_inc(xn_ready, 1)

            def split_piece(j, n):
                dve.wait_ge(xh_ready, n + 1)
                for h in range(H):
                    last = ve.tensor_tensor(XL[:, h, ds(j * CH, CH)], XNF[:, h, :], XH[:, h, ds(j * CH, CH)],
                                            ALU.subtract)
                last.then_inc(xl_ready, 1)

            def maxima(i, q, sigma, bank):
                dve.wait_ge(st_ready, sigma + 1)
                ve.tensor_reduce(mx[:, i, ds(q, 1)], ST[:, bank, :], axis=AX.X, op=ALU.max).then_inc(st_bank_free, 1)

            def max_pair(c):
                dve.wait_ge(st_bank_free, 2 + (c + 1) * T)
                ve.tensor_reduce(mxc[:, :], mx[:, :, :], axis=AX.X, op=ALU.max).then_inc(max_step, 1)
                dve.wait_ge(max_step, 2 * c + 1)
                ve.tensor_scalar(mpair[:, :, 0], mxc[:, :], -1.0 / ROWM, None, ALU.mult).then_inc(max_step, 1)
                dve.wait_ge(max_step, 2 * c + 2)
                ve.scalar_tensor_tensor(mpair[:, :, 1], mpair[:, :, 0], -ROWM, mxc[:, :],
                                        ALU.mult, ALU.subtract).then_inc(mpair_ready, 1)

            def low_part(c, g, half, k):
                dve.wait_ge(exp_done, c * T + GRP * g + k + 1)
                slot = half * GRP + k
                ve.tensor_tensor(PL[:, slot, :], PF[:, slot, :], PH[:, slot, :], ALU.subtract).then_inc(pl_ready, 1)

            def chunk(b, j, more):
                c = b * NCH + j
                for g in range(2):
                    for k in range(GRP):
                        w = 2 * (GRP * g + k)
                        if more:
                            maxima(w % MT, w // MT, (c + 1) * T + w, 0)
                        low_part(c, g + 1, (g + 1) % 2, k)
                        if more:
                            maxima(w % MT + 1, w // MT, (c + 1) * T + w + 1, 1)
                with dve.Fori(1, T // RING - 1) as p:
                    for half in range(2):
                        g = 2 * p + half
                        for k in range(GRP):
                            if more:
                                maxima(k, g + 2, (c + 1) * T + RING + GRP * g + k, k % 2)
                            low_part(c, g + 1, 1 - half, k)
                if more:
                    max_pair(c + 1)
                dve.wait_ge(norm_in, 16 * (c + 1))
                for k in range(GRP):
                    low_part(c, NCH - 1, 1, k)
                    if k == 0:
                        dve.wait_ge(coefs_ready, b + 2)
                        normalise_piece(lambda h: xin_norm[:, h, :], NCH + c)
                    if k == 1:
                        dve.wait_ge(stat_in, 16 * (c + 1))
                        for h in range(H):
                            last = ve.bn_stats(stats[:, h, ds(j, 1), :], xin_stat[:, h, :])
                        last.then_inc(stats_done, 1)
                    if k == 2:
                        split_piece(j, NCH + c)
                for i in range(MT):
                    if more:
                        low_part(c + 1, 0, 0, i)
                    dve.wait_ge(o_ready, c * MT + i + 1)
                    ve.reciprocal(rden[:, i:i + 1], O[:, i, C:C + 1]).then_inc(rden_ready, 1)
                    dve.wait_ge(rden_ready, c * MT + i + 1)
                    ve.tensor_scalar(OSB[:, i, :], O[:, i, 0:C], rden[:, i:i + 1], gam[:, :],
                                     ALU.mult, ALU.mult).then_inc(osb_ready, 1)
                dve.wait_ge(res_ready, 2 * c + 3)
                dve.wait_ge(ot_ready, c + 1)
                for h in range(H):
                    ve.tensor_tensor(RES[:, h, :], ST[:, h, :], RES[:, h, :], ALU.add).then_inc(out_ready, 1)

            ve.memset(cm[:, :], 0.0).then_inc(st_bank_free, 1)
            ve.memset(cv[:, :], 1.0).then_inc(st_bank_free, 1)
            for k in range(MT):
                ve.memset(mpair[:, k, :], 0.0).then_inc(proj_bank_free, 1)
            for k, credited in enumerate((xl_ready, out_ready, res_ready, out_stored)):
                ve.memset(rden[:, k:k + 1], 0.0).then_inc(credited, 1)
            for q in range(4):
                dve.wait_ge(x0_in[q], 16)
                for a in range(q * NCH // 4, (q + 1) * NCH // 4):
                    for h in range(H):
                        last = ve.bn_stats(stats[:, h, a, :], x0[:, h, a * CH:(a + 1) * CH])
            last.then_inc(stats_done, 1)
            dve.wait_ge(stats_done, 1)
            coefficients(0)
            dve.wait_ge(coefs_ready, 1)
            dve.wait_ge(w_hi, 1)
            ve.tensor_tensor(wqkl[:, :, :], wqk[:, :, :], wqkh[:, :, :], ALU.subtract).then_inc(w_split, 1)
            ve.tensor_tensor(wvl[:, :, :], wv[:, :, :], wvh[:, :, :], ALU.subtract).then_inc(w_split, 1)
            with dve.Fori(0, NCH) as j:
                normalise_piece(lambda h: x0[:, h, ds(j * CH, CH)], j)
                split_piece(j, j)
            x1 = PF[:, :, :].rearrange("p r n -> p (r n)").rearrange("p (h n) -> p h n", h=H)
            for half in range(2):
                dve.wait_ge(x1_in, 16 * (half + 1))
                for a in range(NCH // 2):
                    for h in range(H):
                        last = ve.bn_stats(stats[:, h, half * NCH // 2 + a, :], x1[:, h, a * CH:(a + 1) * CH])
                last.then_inc(x1_stats, 1)
            dve.wait_ge(x1_stats, 2)

            with dve.Fori(0, BATCH) as b:
                with dve.Fori(0, NCH // MT) as r:
                    for k in range(MT):
                        i = MT * r + k
                        n = ds(i * CH, CH)
                        dve.wait_ge(proj_hi, b * PROJ + i + 1)
                        ve.tensor_tensor(FL[:, n], O[0:CQ, k, :], F1[0:CQ, n], ALU.subtract)
                        ve.tensor_tensor(G2[CQ:P, n], O[CQ:P, k, :], G1[CQ:P, n],
                                         ALU.subtract).then_inc(proj_bank_free, 1)
                with dve.Fori(0, T // MT) as r:
                    for k in range(MT):
                        i = MT * r + k
                        dve.wait_ge(proj_hi, b * PROJ + NCH + i + 1)
                        ve.tensor_tensor(V[:, ds(i * VW + VL0, C)], O[:, k, 0:C], V[:, ds(i * VW, C)],
                                         ALU.subtract).then_inc(proj_bank_free, 1)
                        maxima(k, r, b * NCH * T + i, k % 2)
                max_pair(b * NCH)
                for k in range(GRP):
                    low_part(b * NCH, 0, 0, k)
                dve.wait_ge(stats_done, b * NCH + 1)
                ve.tensor_scalar(rscale[:, :], nrstd[:, 0:H], 1.0, None, ALU.add)
                ve.scalar_tensor_tensor(rbias[:, :], nmean[:, 0:H], -1.0, nrstd[:, 0:H], ALU.mult, ALU.mult)
                coefficients(b + 1)
                with dve.Fori(0, NCH - 1) as j:
                    chunk(b, j, True)
                chunk(b, NCH - 1, False)


def kernel(**inputs):
    import numpy as np
    import concourse.bacc as bacc
    from concourse.bass_utils import run_bass_kernel_spmd

    f32 = mybir.dt.float32
    x = np.ascontiguousarray(inputs["x"])
    b, c, hh, ww = x.shape
    arrays = {
        "x": x.reshape(b, c, hh * ww),
        "wqT": np.ascontiguousarray(np.transpose(inputs["L0_conv_Wq"])),
        "wkT": np.ascontiguousarray(np.transpose(inputs["L0_conv_Wk"])),
        "wvT": np.ascontiguousarray(np.transpose(inputs["L0_conv_Wv"])),
        "gamma": np.ascontiguousarray(np.broadcast_to(np.asarray(inputs["L0_conv_gamma"]).reshape(1, 1), (128, 1))),
    }
    nc = bacc.Bacc("TRN2", target_bir_lowering=False, num_devices=1)
    args = [nc.dram_tensor(n, a.shape, f32, kind="ExternalInput").ap() for n, a in arrays.items()]
    out = nc.dram_tensor("out", (b, c, hh * ww), f32, kind="ExternalOutput").ap()
    groupnorm_attention(nc, *args, out)
    r = run_bass_kernel_spmd(nc, [arrays], core_ids=[0])
    return r.results[0]["out"].reshape(b, c, hh, ww)
```

```python
import concourse.bass as bass
from concourse import mybir
from contextlib import ExitStack


def groupnorm_attention(nc, x, wqT, wkT, wvT, gamma, out):
    f32, f16, i32 = mybir.dt.float32, mybir.dt.float16, mybir.dt.int32
    ALU, ACT, AX = mybir.AluOpType, mybir.ActivationFunctionType, mybir.AxisListType

    BATCH, C, N = x.shape
    P = 128
    H = C // P
    CQ = wqT.shape[1]
    CH = 512
    NCH = N // CH
    T = N // P
    NPC = 4
    PC = N // NPC
    MT = CH // P
    GRP = 4
    RING = 2 * GRP
    VW = C + 2 + C
    VL0 = C + 2
    GN = 8
    NG = 32 // GN
    PROJ = NCH + T
    VR = 3
    EPS = 1e-5
    SHIFT = 8.0
    ROWM = 64.0
    RSQRT_GUESS = 0x5F3759DF
    COEF = 22
    assert 2 * CQ == P and C == H * P and T == 32 and NCH == 8 and T == VR * NCH + 8

    xv = x.rearrange("b (h p) n -> b p h n", p=P)
    ov = out.rearrange("b (h p) n -> b p h n", p=P)

    with ExitStack() as ctx:
        def sb(name, shape, dt):
            return ctx.enter_context(nc.sbuf_tensor(name, shape, dt))

        def sem(name):
            return ctx.enter_context(nc.semaphore(name))

        F1 = sb("F1", [P, N], f16)
        F2 = sb("F2", [P, N], f16)
        G1 = sb("G1", [P, N], f16)
        G2 = sb("G2", [P, N], f16)
        FL = sb("FL", [CQ, N], f16)
        V = sb("V", [P, T * VW], f16)
        XH = sb("XH", [P, H, N], f16)
        XL = sb("XL", [P, H, N], f16)
        wqk = sb("wqk", [P, H, P], f32)
        wv = sb("wv", [P, H, C], f32)
        wqkh = sb("wqkh", [P, H, P], f16)
        wqkl = sb("wqkl", [P, H, P], f16)
        wvh = sb("wvh", [P, H, C], f16)
        wvl = sb("wvl", [P, H, C], f16)
        gam = sb("gam", [P, 1], f32)
        ident = sb("ident", [P, P], f32)
        ident16 = sb("ident16", [P, P], f16)
        PF = sb("PF", [P, RING, CH], f32)
        PH = sb("PH", [P, RING, CH], f16)
        PL = sb("PL", [P, RING, CH], f16)
        OSB = sb("OSB", [P, MT, C], f32)
        RES = sb("RES", [P, H, CH], f32)
        x0 = sb("x0", [P, H, N], f32)
        xin = sb("xin", [P, H, PC], f32)
        xin_res = sb("xin_res", [P, H, CH], f32)
        XNF = sb("XNF", [P, H, PC], f32)
        mx = sb("mx", [P, MT, NCH], f32)
        mxc = sb("mxc", [P, MT], f32)
        mpair = sb("mpair", [P, MT, 2], f16)
        rden = sb("rden", [P, MT], f32)
        stats = sb("stats", [P, H, NCH, 6], f32)
        mv = sb("mv", [P, H, 2], f32)
        cm = sb("cm", [P, 32], f32)
        cv = sb("cv", [P, 32], f32)
        tm = sb("tm", [P, NG, GN], f32)
        tv = sb("tv", [P, NG, GN], f32)
        gmean = sb("gmean", [P, NG], f32)
        gvar = sb("gvar", [P, NG], f32)
        gr = sb("gr", [P, NG], f32)
        gt = sb("gt", [P, NG], f32)
        bm = sb("bm", [P, NG, GN], f32)
        br = sb("br", [P, NG, GN], f32)
        nmean = sb("nmean", [P, 32], f32)
        nrstd = sb("nrstd", [P, 32], f32)
        rscale = sb("rscale", [P, H], f32)
        rbias = sb("rbias", [P, H], f32)

        O = ctx.enter_context(nc.psum_tensor("O", [P, MT, 512], f32))
        S = ctx.enter_context(nc.psum_tensor("S", [P, 2, 512], f32))
        ST = ctx.enter_context(nc.psum_tensor("ST", [P, 2, 512], f32))

        w_in = sem("w_in")
        x0_in = [sem(f"x0_in{i}") for i in range(4)]
        xin_in = sem("xin_in")
        res_in = sem("res_in")
        fg_moved = [sem("fg_moved0"), sem("fg_moved1")]
        out_stored = sem("out_stored")
        consts = sem("consts")
        w_split = sem("w_split")
        w_hi = sem("w_hi")
        xin_read = sem("xin_read")
        res_coefs = sem("res_coefs")
        coef_step = sem("coef_step")
        coefs_ready = sem("coefs_ready")
        x0_normal = sem("x0_normal")
        xn_ready = sem("xn_ready")
        xh_ready = sem("xh_ready")
        xl_ready = [sem("xl_ready0"), sem("xl_ready1")]
        proj_ready = sem("proj_ready")
        proj_hi = sem("proj_hi")
        proj_bank_free = sem("proj_bank_free")
        st_ready = sem("st_ready")
        st_bank_free = sem("st_bank_free")
        max_step = sem("max_step")
        mpair_ready = sem("mpair_ready")
        mrow_psum = sem("mrow_psum")
        mrow_ready = sem("mrow_ready")
        s_ready = sem("s_ready")
        exp_done = sem("exp_done")
        pl_ready = sem("pl_ready")
        o_ready = sem("o_ready")
        rden_ready = sem("rden_ready")
        osb_ready = sem("osb_ready")
        ot_ready = sem("ot_ready")
        res_ready = sem("res_ready")
        out_ready = sem("out_ready")

        block = ctx.enter_context(nc.Block())
        ds = bass.ds

        @block.sync
        def _(sp):
            for q in range(4):
                sp.dma_start(x0[:, :, q * N // 4:(q + 1) * N // 4],
                             xv[0, :, :, q * N // 4:(q + 1) * N // 4]).then_inc(x0_in[q], 16)
            sp.dma_start(wqk[:, :, 0:CQ], wqT.rearrange("(h p) q -> p h q", p=P)).then_inc(w_in, 16)
            sp.dma_start(wqk[:, :, CQ:P], wkT.rearrange("(h p) q -> p h q", p=P)).then_inc(w_in, 16)
            sp.dma_start(wv[:, :, :], wvT.rearrange("(h p) v -> p h v", p=P)).then_inc(w_in, 16)
            sp.dma_start(gam[:, :], gamma).then_inc(w_in, 16)
            with sp.Fori(0, BATCH) as b:
                for half in range(2):
                    sp.wait_ge(proj_bank_free, b * PROJ + 4 + 4 * (half + 1))
                    cols = slice(half * N // 2, (half + 1) * N // 2)
                    sp.dma_start(F1[CQ:P, cols], FL[:, cols]).then_inc(fg_moved[half], 16)
                    sp.dma_start(F2[CQ:P, cols], F1[0:CQ, cols]).then_inc(fg_moved[half], 16)
                    sp.dma_start(G1[0:CQ, cols], G1[CQ:P, cols]).then_inc(fg_moved[half], 16)
                after = sp.snap((b + 1) % BATCH)
                for norm in range(2):
                    with sp.Fori(norm * NPC, (norm + 1) * NPC) as j:
                        c = b * NCH + j
                        sp.wait_ge(res_ready, 2 * c + 1)
                        sp.dma_start(xin_res[:, :, :], xv[b, :, :, ds(j * CH, CH)]).then_inc(res_in, 16)
                        if norm:
                            sp.wait_ge(xin_read, b * NPC + NPC + 2)
                            sp.wait_ge(xn_ready, b * NPC + j - NPC + 1)
                        else:
                            sp.wait_ge(xn_ready, b * NPC + 1)
                            sp.wait_ge(xin_read, b * NPC + j + 2)
                        sp.dma_start(xin[:, :, :],
                                     xv[after, :, :, ds((j - norm * NPC) * PC, PC)]).then_inc(xin_in, 16)
                        sp.wait_ge(out_ready, 2 * c + 3)
                        sp.dma_start(ov[b, :, :, ds(j * CH, CH)], RES[:, :, :]).then_inc(out_stored, 16)
            sp.wait_ge(out_stored, 16 * BATCH * NCH + 1)

        @block.gpsimd
        def _(pool):
            pool.memset(F2[0:CQ, :], 0.0).then_inc(consts, 1)
            pool.memset(G2[0:CQ, :], 0.0).then_inc(consts, 1)
            pool.memset(V[:, :].rearrange("p (t w) -> p t w", w=VW)[:, :, C:C + 1], 1.0).then_inc(consts, 1)
            pool.memset(ident[:, :], 0.0).then_inc(consts, 1)
            pool.memset(ident16[:, :], 0.0).then_inc(consts, 1)
            pool.wait_ge(consts, 5)
            pool.memset(F2[0:2, :], 1.0).then_inc(consts, 1)
            pool.wait_ge(consts, 6)
            pool.memset(F2[0:1, :], ROWM).then_inc(consts, 1)
            for m in (ident, ident16):
                pool.affine_select(out=m[:, :], in_=m[:, :], compare_op=ALU.not_equal, fill=1.0,
                                   base=0, pattern=[[-1, P]], channel_multiplier=1).then_inc(consts, 1)
            for q in range(NPC):
                pool.wait_ge(xh_ready, 2 * q + 2)
                cols = slice(q * PC, (q + 1) * PC)
                pool.tensor_tensor(XL[:, 1, cols], x0[:, 1, cols], XH[:, 1, cols], ALU.subtract).then_inc(xl_ready[1], 1)

        @block.tensor
        def _(pe):
            mm = nc.tensor.matmul

            def transposed_scores(j, i, q, sigma, bank):
                pe.wait_ge(st_bank_free, sigma + 1)
                mm(ST[:, bank, :], G1[:, ds(j * CH + i * P, P)], F1[:, ds(q * CH, CH)],
                   start=True, stop=True).then_inc(st_ready, 1)

            def scores(j, t, bank):
                mm(S[:, bank, :], F1[:, ds(t * P, P)], G1[:, ds(j * CH, CH)], start=True, stop=False)
                mm(S[:, bank, :], F2[:, ds(t * P, P)], G2[:, ds(j * CH, CH)],
                   start=False, stop=True).then_inc(s_ready, 1)

            def weigh(t, slot, i, first=False, last=False):
                ph = PH[:, slot, i * P:(i + 1) * P]
                mm(O[:, i, 0:C + 1], ph, V[:, ds(t * VW, C + 1)], start=first, stop=False)
                mm(O[:, i, 0:C], ph, V[:, ds(t * VW + VL0, C)], start=False, stop=False)
                return mm(O[:, i, 0:C + 1], PL[:, slot, i * P:(i + 1) * P], V[:, ds(t * VW, C + 1)],
                          start=False, stop=last)

            def maxima_to_rows(c):
                pe.wait_ge(mpair_ready, c + 1)
                for i in range(MT):
                    m = mm(ST[0:2, 0, i * P:(i + 1) * P], mpair[:, i, :], ident16[:, :], start=True, stop=True)
                m.then_inc(mrow_psum, 1)

            def group(j, c, g, half, first=False, st=0):
                for k in range(GRP):
                    t = GRP * g + k
                    tau = c * T + t
                    pe.wait_ge(exp_done, tau + GRP - 1)
                    scores(j, t + GRP, k % 2)
                    pe.wait_ge(pl_ready, tau + 1)
                    for i in range(MT):
                        weigh(t, half * GRP + k, i, first=first and k == 0)
                        if first and st and k == 0 and i == 1:
                            pe.wait_ge(out_ready, 2 * c + 1)
                        if st == 2 and i % 2:
                            w = 2 * k + i // 2
                            transposed_scores(j + 1, w % MT, 2 * g + w // MT,
                                              (c + 1) * T + 2 * t + i // 2, i // 2)
                        if st == 1 and i == 1:
                            transposed_scores(j + 1, k, g + 2, (c + 1) * T + RING + t, k % 2)

            def chunk(b, j, more):
                c = b * NCH + j
                group(j, c, 0, 0, first=True, st=2 * more)
                group(j, c, 1, 1, st=2 * more)
                with pe.Fori(1, T // RING - 1) as p:
                    group(j, c, 2 * p, 0, st=1 * more)
                    group(j, c, 2 * p + 1, 1, st=1 * more)
                for k in range(GRP):
                    t = T - RING + k
                    if more and k == 2:
                        maxima_to_rows(c + 1)
                    pe.wait_ge(exp_done, c * T + t + GRP - 1)
                    scores(j, t + GRP, k % 2)
                    pe.wait_ge(pl_ready, c * T + t + 1)
                    for i in range(MT):
                        weigh(t, k, i)
                if more:
                    pe.wait_ge(mrow_ready, c + 2)
                for i in range(MT):
                    for k in range(GRP):
                        t = T - GRP + k
                        if i == 0:
                            pe.wait_ge(pl_ready, c * T + t + 1)
                        w = weigh(t, GRP + k, i, last=k == GRP - 1)
                    w.then_inc(o_ready, 1)
                    if more:
                        pe.wait_ge(exp_done, c * T + T + i - 1)
                        scores(j + 1, i, i % 2)
                pe.wait_ge(out_ready, 2 * c + 1)
                for i in range(MT):
                    pe.wait_ge(osb_ready, c * MT + i + 1)
                    for h in range(H):
                        m = nc.tensor.transpose(ST[:, h, i * P:(i + 1) * P], OSB[:, i, h * P:(h + 1) * P],
                                                ident[:, :])
                m.then_inc(ot_ready, 1)

            pe.wait_ge(consts, 9)
            pe.wait_ge(w_split, 2)
            with pe.Fori(0, BATCH) as b:
                with pe.Fori(0, NCH // MT) as r:
                    for k in range(MT):
                        i = MT * r + k
                        n = ds(i * CH, CH)
                        for h in range(H):
                            pe.wait_ge(xl_ready[h], b * NPC + 2 * r + k // 2 + 1)
                        pe.wait_ge(proj_bank_free, b * PROJ + i + 1)
                        for h in range(H):
                            mm(O[:, k, :], wqkh[:, h, :], XH[:, h, n], start=h == 0, stop=False)
                            mm(O[:, k, :], wqkl[:, h, :], XH[:, h, n], start=False, stop=False)
                            m = mm(O[:, k, :], wqkh[:, h, :], XL[:, h, n], start=False, stop=h == H - 1)
                        m.then_inc(proj_ready, 1)
                def values(i, k, lag):
                    pe.wait_ge(proj_bank_free, b * PROJ + NCH + i + MT - lag + 1)
                    for h in range(H):
                        xh, xl = XH[:, h, ds(i * P, P)], XL[:, h, ds(i * P, P)]
                        mm(O[:, k, 0:C], xh, wvh[:, h, :], start=h == 0, stop=False)
                        mm(O[:, k, 0:C], xh, wvl[:, h, :], start=False, stop=False)
                        m = mm(O[:, k, 0:C], xl, wvh[:, h, :], start=False, stop=h == H - 1)
                    m.then_inc(proj_ready, 1)

                for half in range(2):
                    with pe.Fori(half * NCH // 2, (half + 1) * NCH // 2) as r:
                        for k in range(MT):
                            if k < VR:
                                values(VR * r + k, k, VR)
                            if k == 0:
                                pe.wait_ge(out_ready, 2 * NCH * b + 1)
                                pe.wait_ge(fg_moved[half], 48 * (b + 1))
                            transposed_scores(0, k, r, b * NCH * T + MT * r + k, k % 2)
                for i in range(4):
                    values(VR * NCH + i, i, VR)
                maxima_to_rows(b * NCH)
                for k in range(GRP):
                    if k % 2 == 0:
                        values(VR * NCH + 4 + k, k, MT)
                        values(VR * NCH + 5 + k, k + 1, MT)
                    if k == 0:
                        pe.wait_ge(mrow_ready, b * NCH + 1)
                    if k >= 2:
                        pe.wait_ge(exp_done, b * NCH * T + k - 1)
                    if k == GRP - 1:
                        pe.wait_ge(proj_bank_free, (b + 1) * PROJ + MT)
                    scores(0, k, k % 2)
                with pe.Fori(0, NCH - 1) as j:
                    chunk(b, j, True)
                chunk(b, NCH - 1, False)

        @block.scalar
        def _(act):
            def exps(c, g, half, k):
                act.wait_ge(s_ready, c * T + GRP * g + k + 1)
                slot = half * GRP + k
                nc.scalar.activation(PH[:, slot, :], S[:, k % 2, :], ACT.Exp, bias=SHIFT)
                nc.scalar.activation(PF[:, slot, :], S[:, k % 2, :], ACT.Exp, bias=SHIFT).then_inc(exp_done, 1)

            def chunk(b, j, more, norm):
                c = b * NCH + j
                for k in range(GRP):
                    exps(c, 1, 1, k)
                with act.Fori(1, T // RING - 1) as p:
                    for k in range(GRP):
                        exps(c, 2 * p, 0, k)
                    for k in range(GRP):
                        exps(c, 2 * p + 1, 1, k)
                for k in range(GRP):
                    exps(c, NCH - 2, 0, k)
                for k in range(GRP):
                    exps(c, NCH - 1, 1, k)
                    if k < 2:
                        if k == 0:
                            act.wait_ge(res_coefs, b + 1)
                            act.wait_ge(res_in, 16 * (c + 1))
                            act.wait_ge(out_stored, 16 * c + 1)
                        nc.scalar.activation(RES[:, k, :], xin_res[:, k, :], ACT.Identity,
                                             scale=rscale[:, k:k + 1], bias=rbias[:, k:k + 1]).then_inc(res_ready, 1)
                    elif norm:
                        if k == 2:
                            act.wait_ge(xn_ready, b * NPC + j - NPC + 2)
                        nc.scalar.copy(XH[:, k - 2, ds((j - NPC) * PC, PC)], XNF[:, k - 2, :]).then_inc(xh_ready, 1)
                if more:
                    act.wait_ge(mrow_psum, c + 2)
                    nc.scalar.copy(G2[0:2, ds((j + 1) * CH, CH)], ST[0:2, 0, :]).then_inc(mrow_ready, 1)
                    for k in range(GRP):
                        exps(c + 1, 0, 0, k)

            act.wait_ge(w_in, 64)
            nc.scalar.copy(wqkh[:, :, :], wqk[:, :, :])
            nc.scalar.copy(wvh[:, :, :], wv[:, :, :]).then_inc(w_hi, 1)
            for q in range(NPC):
                act.wait_ge(x0_normal, q + 1)
                for h in range(H):
                    nc.scalar.copy(XH[:, h, q * PC:(q + 1) * PC], x0[:, h, q * PC:(q + 1) * PC]).then_inc(xh_ready, 1)
            with act.Fori(0, BATCH) as b:
                def round_values(i, k):
                    act.wait_ge(proj_ready, b * PROJ + NCH + i + 1)
                    nc.scalar.copy(V[:, ds(i * VW, C)], O[:, k, 0:C]).then_inc(proj_hi, 1)

                with act.Fori(0, NCH // MT) as r:
                    for k in range(MT):
                        i = MT * r + k
                        n = ds(i * CH, CH)
                        act.wait_ge(proj_ready, b * PROJ + i + 1)
                        nc.scalar.copy(F1[0:CQ, n], O[0:CQ, k, :])
                        nc.scalar.copy(G1[CQ:P, n], O[CQ:P, k, :]).then_inc(proj_hi, 1)
                with act.Fori(0, NCH) as r:
                    for k in range(VR):
                        round_values(VR * r + k, k)
                for i in range(4):
                    round_values(VR * NCH + i, i)
                act.wait_ge(mrow_psum, b * NCH + 1)
                nc.scalar.copy(G2[0:2, 0:CH], ST[0:2, 0, :]).then_inc(mrow_ready, 1)
                for k in range(GRP):
                    if k % 2 == 0:
                        round_values(VR * NCH + 4 + k, k)
                        round_values(VR * NCH + 5 + k, k + 1)
                    exps(b * NCH, 0, 0, k)
                with act.Fori(0, NPC) as j:
                    chunk(b, j, True, False)
                with act.Fori(NPC, NCH - 1) as j:
                    chunk(b, j, True, True)
                chunk(b, NCH - 1, False, True)

        @block.vector
        def _(dve):
            ve = nc.vector

            def coefficients(n):
                base = n * COEF
                done = [0]

                def step(ins):
                    done[0] += 1
                    ins.then_inc(coef_step, 1)
                    dve.wait_ge(coef_step, base + done[0])

                for h in range(H):
                    last = ve.bn_aggr(mv[:, h, :], stats[:, h, :, :].rearrange("p a b -> p (a b)"))
                step(last)
                ve.tensor_copy(cm[:, 0:H], mv[:, :, 0])
                step(ve.tensor_copy(cv[:, 0:H], mv[:, :, 1]))
                flat = "p a b -> p (a b)"
                ve.transpose(tm[:, :, :].rearrange(flat), cm[:, :])
                step(ve.transpose(tv[:, :, :].rearrange(flat), cv[:, :]))
                step(ve.tensor_reduce(gmean[:, :], tm[:, :, :], axis=AX.X, op=ALU.add))
                step(ve.tensor_scalar(gmean[:, :], gmean[:, :], 1.0 / GN, None, ALU.mult))
                spread = gmean[:, :].unsqueeze(2).to_broadcast([P, NG, GN])
                ve.tensor_copy(bm[:, :, :], spread)
                step(ve.tensor_tensor(tm[:, :, :], tm[:, :, :], spread, ALU.subtract))
                step(ve.tensor_tensor(tm[:, :, :], tm[:, :, :], tm[:, :, :], ALU.mult))
                step(ve.tensor_tensor(tv[:, :, :], tv[:, :, :], tm[:, :, :], ALU.add))
                step(ve.tensor_reduce(gvar[:, :], tv[:, :, :], axis=AX.X, op=ALU.add))
                step(ve.tensor_scalar(gvar[:, :], gvar[:, :], 1.0 / GN, EPS, ALU.mult, ALU.add))
                step(ve.tensor_scalar(gt[:, :].bitcast(i32), gvar[:, :].bitcast(i32), 1, None,
                                      ALU.logical_shift_right))
                step(ve.tensor_scalar(gr[:, :].bitcast(i32), gt[:, :].bitcast(i32), -1.0, float(RSQRT_GUESS),
                                      ALU.mult, ALU.add))
                for _ in range(3):
                    step(ve.scalar_tensor_tensor(gt[:, :], gr[:, :], -0.5, gr[:, :], ALU.mult, ALU.mult))
                    step(ve.tensor_tensor(gt[:, :], gt[:, :], gvar[:, :], ALU.mult))
                    step(ve.scalar_tensor_tensor(gr[:, :], gt[:, :], 1.5, gr[:, :], ALU.add, ALU.mult))
                ve.transpose(nmean[:, :], bm[:, :, :].rearrange(flat))
                step(ve.tensor_copy(br[:, :, :], gr[:, :].unsqueeze(2).to_broadcast([P, NG, GN])))
                assert done[0] == COEF
                ve.transpose(nrstd[:, :], br[:, :, :].rearrange(flat)).then_inc(coefs_ready, 1)

            def normalise(dst, src, h):
                return ve.tensor_scalar(dst, src, nmean[:, h:h + 1], nrstd[:, h:h + 1], ALU.subtract, ALU.mult)

            def maxima(i, q, sigma, bank):
                dve.wait_ge(st_ready, sigma + 1)
                ve.tensor_reduce(mx[:, i, ds(q, 1)], ST[:, bank, :], axis=AX.X, op=ALU.max).then_inc(st_bank_free, 1)

            def max_pair(c):
                dve.wait_ge(st_bank_free, 2 + (c + 1) * T)
                ve.tensor_reduce(mxc[:, :], mx[:, :, :], axis=AX.X, op=ALU.max).then_inc(max_step, 1)
                dve.wait_ge(max_step, 2 * c + 1)
                ve.tensor_scalar(mpair[:, :, 0], mxc[:, :], -1.0 / ROWM, None, ALU.mult).then_inc(max_step, 1)
                dve.wait_ge(max_step, 2 * c + 2)
                ve.scalar_tensor_tensor(mpair[:, :, 1], mpair[:, :, 0], -ROWM, mxc[:, :],
                                        ALU.mult, ALU.subtract).then_inc(mpair_ready, 1)

            def low_part(c, g, half, k):
                dve.wait_ge(exp_done, c * T + GRP * g + k + 1)
                slot = half * GRP + k
                ve.tensor_tensor(PL[:, slot, :], PF[:, slot, :], PH[:, slot, :], ALU.subtract).then_inc(pl_ready, 1)

            def chunk(b, j, more, norm):
                c = b * NCH + j
                for g in range(2):
                    for k in range(GRP):
                        w = 2 * (GRP * g + k)
                        if more:
                            maxima(w % MT, w // MT, (c + 1) * T + w, 0)
                        low_part(c, g + 1, (g + 1) % 2, k)
                        if more:
                            maxima(w % MT + 1, w // MT, (c + 1) * T + w + 1, 1)
                with dve.Fori(1, T // RING - 1) as p:
                    for half in range(2):
                        g = 2 * p + half
                        for k in range(GRP):
                            if more:
                                maxima(k, g + 2, (c + 1) * T + RING + GRP * g + k, k % 2)
                            low_part(c, g + 1, 1 - half, k)
                if more:
                    max_pair(c + 1)
                n = NPC * (b + 1) + j - NPC
                for k in range(GRP):
                    low_part(c, NCH - 1, 1, k)
                    if k == 0:
                        dve.wait_ge(xin_in, 16 * (c + 1))
                    if k < 2 and not norm:
                        for h in range(H):
                            last = ve.bn_stats(stats[:, h, ds(2 * j + k, 1), :], xin[:, h, k * CH:(k + 1) * CH])
                        if k == 1:
                            last.then_inc(xin_read, 1)
                    if k == 0 and norm:
                        dve.wait_ge(coefs_ready, b + 2)
                        dve.wait_ge(xl_ready[1], n)
                        for h in range(H):
                            last = normalise(XNF[:, h, :], xin[:, h, :], h)
                        last.then_inc(xn_ready, 1)
                for i in range(MT):
                    dve.wait_ge(o_ready, c * MT + i + 1)
                    ve.reciprocal(rden[:, i:i + 1], O[:, i, C:C + 1]).then_inc(rden_ready, 1)
                    dve.wait_ge(rden_ready, c * MT + i + 1)
                    ve.tensor_scalar(OSB[:, i, :], O[:, i, 0:C], rden[:, i:i + 1], gam[:, :],
                                     ALU.mult, ALU.mult).then_inc(osb_ready, 1)
                    if more:
                        low_part(c + 1, 0, 0, i)
                    if norm and i < H:
                        dve.wait_ge(xh_ready, 2 * n + i + 1)
                        cols = ds((j - NPC) * PC, PC)
                        ve.tensor_tensor(XL[:, i, cols], XNF[:, i, :], XH[:, i, cols],
                                         ALU.subtract).then_inc(xl_ready[i], 1)
                dve.wait_ge(res_ready, 2 * c + 3)
                dve.wait_ge(ot_ready, c + 1)
                for h in range(H):
                    ve.tensor_tensor(RES[:, h, :], ST[:, h, :], RES[:, h, :], ALU.add).then_inc(out_ready, 1)

            ve.memset(cm[:, :], 0.0).then_inc(st_bank_free, 1)
            ve.memset(cv[:, :], 1.0).then_inc(st_bank_free, 1)
            for k in range(MT):
                ve.memset(mpair[:, k, :], 0.0).then_inc(proj_bank_free, 1)
            ve.memset(gmean[:, :], 0.0).then_inc(xn_ready, 1)
            for k, credited in enumerate((xin_read, out_ready, res_ready, out_stored)):
                ve.memset(rden[:, k:k + 1], 0.0).then_inc(credited, 1)
            for q in range(NPC):
                dve.wait_ge(x0_in[q], 16)
                for a in range(q * PC // CH, (q + 1) * PC // CH):
                    for h in range(H):
                        last = ve.bn_stats(stats[:, h, a, :], x0[:, h, a * CH:(a + 1) * CH])
            last.then_inc(xin_read, 1)
            dve.wait_ge(xin_read, 2)
            coefficients(0)
            dve.wait_ge(coefs_ready, 1)
            for q in range(NPC + 1):
                if q < NPC:
                    for h in range(H):
                        last = normalise(x0[:, h, q * PC:(q + 1) * PC], x0[:, h, q * PC:(q + 1) * PC], h)
                    last.then_inc(x0_normal, 1)
                if q > 0:
                    dve.wait_ge(xh_ready, 2 * q)
                    cols = slice((q - 1) * PC, q * PC)
                    ve.tensor_tensor(XL[:, 0, cols], x0[:, 0, cols], XH[:, 0, cols],
                                     ALU.subtract).then_inc(xl_ready[0], 1)
                if q == 0:
                    dve.wait_ge(w_hi, 1)
                    ve.tensor_tensor(wqkl[:, :, :], wqk[:, :, :], wqkh[:, :, :], ALU.subtract).then_inc(w_split, 1)
                    ve.tensor_tensor(wvl[:, :, :], wv[:, :, :], wvh[:, :, :], ALU.subtract).then_inc(w_split, 1)

            with dve.Fori(0, BATCH) as b:
                def split_values(i, k):
                    dve.wait_ge(proj_hi, b * PROJ + NCH + i + 1)
                    ve.tensor_tensor(V[:, ds(i * VW + VL0, C)], O[:, k, 0:C], V[:, ds(i * VW, C)],
                                     ALU.subtract).then_inc(proj_bank_free, 1)

                with dve.Fori(0, NCH // MT) as r:
                    for k in range(MT):
                        i = MT * r + k
                        n = ds(i * CH, CH)
                        dve.wait_ge(proj_hi, b * PROJ + i + 1)
                        ve.tensor_tensor(FL[:, n], O[0:CQ, k, :], F1[0:CQ, n], ALU.subtract)
                        ve.tensor_tensor(G2[CQ:P, n], O[CQ:P, k, :], G1[CQ:P, n],
                                         ALU.subtract).then_inc(proj_bank_free, 1)
                with dve.Fori(0, NCH) as r:
                    for k in range(MT):
                        if k < VR:
                            split_values(VR * r + k, k)
                        maxima(k, r, b * NCH * T + MT * r + k, k % 2)
                max_pair(b * NCH)
                for i in range(4):
                    split_values(VR * NCH + i, i)
                for k in range(GRP):
                    if k % 2 == 0:
                        split_values(VR * NCH + 4 + k, k)
                        split_values(VR * NCH + 5 + k, k + 1)
                    low_part(b * NCH, 0, 0, k)
                dve.wait_ge(coefs_ready, b + 1)
                ve.tensor_scalar(rscale[:, :], nrstd[:, 0:H], 1.0, None, ALU.add)
                ve.scalar_tensor_tensor(rbias[:, :], nmean[:, 0:H], -1.0, nrstd[:, 0:H],
                                        ALU.mult, ALU.mult).then_inc(res_coefs, 1)
                with dve.Fori(0, NPC) as j:
                    chunk(b, j, True, False)
                coefficients(b + 1)
                with dve.Fori(NPC, NCH - 1) as j:
                    chunk(b, j, True, True)
                chunk(b, NCH - 1, False, True)


def kernel(**inputs):
    import numpy as np
    import concourse.bacc as bacc
    from concourse.bass_utils import run_bass_kernel_spmd

    f32 = mybir.dt.float32
    x = np.ascontiguousarray(inputs["x"])
    b, c, hh, ww = x.shape
    arrays = {
        "x": x.reshape(b, c, hh * ww),
        "wqT": np.ascontiguousarray(np.transpose(inputs["L0_conv_Wq"])),
        "wkT": np.ascontiguousarray(np.transpose(inputs["L0_conv_Wk"])),
        "wvT": np.ascontiguousarray(np.transpose(inputs["L0_conv_Wv"])),
        "gamma": np.ascontiguousarray(np.broadcast_to(np.asarray(inputs["L0_conv_gamma"]).reshape(1, 1), (128, 1))),
    }
    nc = bacc.Bacc("TRN2", target_bir_lowering=False, num_devices=1)
    args = [nc.dram_tensor(n, a.shape, f32, kind="ExternalInput").ap() for n, a in arrays.items()]
    out = nc.dram_tensor("out", (b, c, hh * ww), f32, kind="ExternalOutput").ap()
    groupnorm_attention(nc, *args, out)
    r = run_bass_kernel_spmd(nc, [arrays], core_ids=[0])
    return r.results[0]["out"].reshape(b, c, hh, ww)
```

```python
import concourse.bass as bass
from concourse import mybir
from contextlib import ExitStack


def groupnorm_attention(nc, x, wqT, wkT, wvT, gamma, out):
    f32, f16, i32 = mybir.dt.float32, mybir.dt.float16, mybir.dt.int32
    ALU, ACT, AX = mybir.AluOpType, mybir.ActivationFunctionType, mybir.AxisListType

    BATCH, C, N = x.shape
    P = 128
    H = C // P
    CQ = wqT.shape[1]
    CH = 512
    NCH = N // CH
    T = N // P
    NPC = 4
    PC = N // NPC
    MT = CH // P
    GRP = 4
    RING = 2 * GRP
    VW = C + 2 + C
    VL0 = C + 2
    GN = 8
    NG = 32 // GN
    PROJ = NCH + T
    VR = 3
    EPS = 1e-5
    SHIFT = 8.0
    RSQRT_GUESS = 0x5F3759DF
    DSUB = 1
    COEF = 22
    COEF_VAR = 10
    assert 2 * CQ == P and C == H * P and T == 32 and NCH == 8 and T == VR * NCH + 8

    xv = x.rearrange("b (h p) n -> b p h n", p=P)
    ov = out.rearrange("b (h p) n -> b p h n", p=P)

    with ExitStack() as ctx:
        def sb(name, shape, dt):
            return ctx.enter_context(nc.sbuf_tensor(name, shape, dt))

        def sem(name):
            return ctx.enter_context(nc.semaphore(name))

        F1 = sb("F1", [P, N], f16)
        G1 = sb("G1", [P, N], f16)
        GL = sb("GL", [P, N], f16)
        V = sb("V", [P, T * VW], f16)
        XH = sb("XH", [P, H, N], f16)
        XL = sb("XL", [P, H, N], f16)
        wqk = sb("wqk", [P, H, P], f32)
        wv = sb("wv", [P, H, C], f32)
        wqkh = sb("wqkh", [P, H, P], f16)
        wqkl = sb("wqkl", [P, H, P], f16)
        wvh = sb("wvh", [P, H, C], f16)
        wvl = sb("wvl", [P, H, C], f16)
        gam = sb("gam", [P, 1], f32)
        ident = sb("ident", [P, P], f32)
        ones = sb("ones", [P, P], f32)
        SC = sb("SC", [P, T * CH], f32)
        PH = sb("PH", [P, RING, CH], f16)
        PL = sb("PL", [P, RING, CH], f16)
        FL = PH[0:CQ, :, :].rearrange("p r m -> p (r m)")
        OSB = sb("OSB", [P, MT, C], f32)
        RES = sb("RES", [P, H, CH], f32)
        x0 = SC[:, 0:H * N].rearrange("p (h n) -> p h n", h=H)
        xin = sb("xin", [P, H, PC], f32)
        xin_res = sb("xin_res", [P, H, CH], f32)
        MX = sb("MX", [P, CH], f32)
        mxc = sb("mxc", [P, MT], f32)
        diag = sb("diag", [P, MT, P], f32)
        MB = sb("MB", [P, CH], f32)
        rden = sb("rden", [P, MT], f32)
        stats = sb("stats", [P, H, NCH, 6], f32)
        mv = sb("mv", [P, H, 2], f32)
        cm = sb("cm", [P, 32], f32)
        cv = sb("cv", [P, 32], f32)
        tm = sb("tm", [P, NG, GN], f32)
        tv = sb("tv", [P, NG, GN], f32)
        gmean = sb("gmean", [P, NG], f32)
        gvar = sb("gvar", [P, NG], f32)
        gr = sb("gr", [P, NG], f32)
        gt = sb("gt", [P, NG], f32)
        bm = sb("bm", [P, NG, GN], f32)
        br = sb("br", [P, NG, GN], f32)
        nmean = sb("nmean", [P, 32], f32)
        nrstd = sb("nrstd", [P, 32], f32)
        rscale = sb("rscale", [P, H], f32)
        rbias = sb("rbias", [P, H], f32)

        O = ctx.enter_context(nc.psum_tensor("O", [P, MT, 512], f32))
        S = ctx.enter_context(nc.psum_tensor("S", [P, 2, 512], f32))
        ST = ctx.enter_context(nc.psum_tensor("ST", [P, 2, 512], f32))

        w_in = sem("w_in")
        x0_in = [sem(f"x0_in{i}") for i in range(4)]
        xin_in = sem("xin_in")
        load_turn = sem("load_turn")
        res_in = sem("res_in")
        fg_moved = [sem("fg_moved0"), sem("fg_moved1")]
        out_stored = sem("out_stored")
        consts = sem("consts")
        w_split = sem("w_split")
        w_hi = sem("w_hi")
        xin_read = sem("xin_read")
        res_coefs = sem("res_coefs")
        coef_step = sem("coef_step")
        coefs_ready = sem("coefs_ready")
        x0_normal = sem("x0_normal")
        xn_ready = sem("xn_ready")
        xh_ready = sem("xh_ready")
        xl_ready = [sem("xl_ready0"), sem("xl_ready1")]
        xl_turn = sem("xl_turn")
        proj_ready = sem("proj_ready")
        proj_hi = sem("proj_hi")
        proj_bank_free = sem("proj_bank_free")
        store_turn = sem("store_turn")
        s_stored = sem("s_stored")
        s_maxed = sem("s_maxed")
        maxt_ready = sem("maxt_ready")
        mxc_ready = sem("mxc_ready")
        diag_ready = sem("diag_ready")
        mb_psum = sem("mb_psum")
        mb_ready = sem("mb_ready")
        sub_turn = sem("sub_turn")
        sub_first = sem("sub_first")
        sub_ready = sem("sub_ready")
        weighed = sem("weighed")
        s_ready = sem("s_ready")
        exp_done = sem("exp_done")
        pl_ready = sem("pl_ready")
        o_ready = sem("o_ready")
        rden_ready = sem("rden_ready")
        osb_ready = sem("osb_ready")
        ot_ready = sem("ot_ready")
        res_ready = sem("res_ready")
        out_ready = sem("out_ready")

        block = ctx.enter_context(nc.Block())
        ds = bass.ds

        @block.sync
        def _(sp):
            for q in range(4):
                sp.dma_start(x0[:, :, q * N // 4:(q + 1) * N // 4],
                             xv[0, :, :, q * N // 4:(q + 1) * N // 4]).then_inc(x0_in[q], 16)
            sp.dma_start(wqk[:, :, 0:CQ], wqT.rearrange("(h p) q -> p h q", p=P)).then_inc(w_in, 16)
            sp.dma_start(wqk[:, :, CQ:P], wkT.rearrange("(h p) q -> p h q", p=P)).then_inc(w_in, 16)
            sp.dma_start(wv[:, :, :], wvT.rearrange("(h p) v -> p h v", p=P)).then_inc(w_in, 16)
            sp.dma_start(gam[:, :], gamma).then_inc(w_in, 16)
            with sp.Fori(0, BATCH) as b:
                for half in range(2):
                    sp.wait_ge(proj_bank_free, b * PROJ + 4 + 4 * (half + 1))
                    cols = slice(half * N // 2, (half + 1) * N // 2)
                    sp.dma_start(F1[CQ:P, cols], FL[:, cols]).then_inc(fg_moved[half], 16)
                    sp.dma_start(G1[0:CQ, cols], G1[CQ:P, cols]).then_inc(fg_moved[half], 16)
                    sp.dma_start(GL[0:CQ, cols], GL[CQ:P, cols]).then_inc(fg_moved[half], 16)
                after = sp.snap((b + 1) % BATCH)
                for norm in range(2):
                    with sp.Fori(norm * NPC, (norm + 1) * NPC) as j:
                        c = b * NCH + j
                        sp.wait_ge(res_ready, 2 * c + 1)
                        sp.dma_start(xin_res[:, :, :], xv[b, :, :, ds(j * CH, CH)]).then_inc(res_in, 16)
                        sp.wait_ge(xin_read, b * NPC + (NPC if norm else j) + 2)
                        sp.sem_inc(load_turn, 1)
                        sp.wait_ge(xl_ready[1], b * NPC + (j if norm else NPC))
                        sp.dma_start(xin[:, :, :],
                                     xv[after, :, :, ds((j - norm * NPC) * PC, PC)]).then_inc(xin_in, 16)
                        sp.wait_ge(out_ready, 2 * c + 4)
                        sp.dma_start(ov[b, :, :, ds(j * CH, CH)], RES[:, :, :]).then_inc(out_stored, 16)
            sp.wait_ge(out_stored, 16 * BATCH * NCH + 1)

        @block.gpsimd
        def _(pool):
            pool.memset(V[:, :].rearrange("p (t w) -> p t w", w=VW)[:, :, C:C + 1], 1.0).then_inc(consts, 1)
            pool.memset(ones[:, :], 1.0).then_inc(consts, 1)
            pool.memset(ident[:, :], 0.0).then_inc(consts, 1)
            pool.wait_ge(consts, 3)
            pool.affine_select(out=ident[:, :], in_=ident[:, :], compare_op=ALU.not_equal, fill=1.0,
                               base=0, pattern=[[-1, P]], channel_multiplier=1).then_inc(consts, 1)
            for q in range(NPC):
                pool.wait_ge(xh_ready, 2 * q + 2)
                cols = slice(q * PC, (q + 1) * PC)
                pool.tensor_tensor(XL[:, 1, cols], x0[:, 1, cols], XH[:, 1, cols], ALU.subtract).then_inc(xl_ready[1], 1)

            def low_input(b, piece):
                for h in range(H):
                    pool.wait_ge(xh_ready, 2 * (NPC * (b + 1) + piece) + h + 1)
                    pool.sem_inc(xl_turn, 1)
                    cols = ds(piece * PC, PC)
                    pool.tensor_tensor(XL[:, h, cols], xin[:, h, :], XH[:, h, cols],
                                       ALU.subtract).then_inc(xl_ready[h], 1)

            def subtract_maxima(c):
                pool.wait_ge(mb_ready, c + 1)
                pool.sem_inc(sub_turn, 1)
                for t in range(DSUB, T):
                    tile = SC[:, t * CH:(t + 1) * CH]
                    pool.tensor_tensor(tile, tile, MB[:, :], ALU.subtract).then_inc(sub_ready, 1)

            with pool.Fori(0, BATCH) as b:
                with pool.Fori(0, NPC + 1) as j:
                    subtract_maxima(b * NCH + j)
                with pool.Fori(NPC + 1, NCH) as j:
                    subtract_maxima(b * NCH + j)
                    low_input(b, j - NPC - 1)
                low_input(b, NPC - 1)

        @block.tensor
        def _(pe):
            mm = nc.tensor.matmul

            def scores(j, c, t, bank):
                pe.wait_ge(s_stored, c * T + t + 1)
                mm(S[:, bank, :], F1[:, ds(t * P, P)], G1[:, ds(j * CH, CH)], start=True, stop=False)
                mm(S[:, bank, :], F1[0:CQ, ds(t * P, P)], GL[0:CQ, ds(j * CH, CH)],
                   start=False, stop=True).then_inc(s_ready, 1)

            def weigh(t, slot, i, first=False, last=False):
                ph = PH[:, slot, i * P:(i + 1) * P]
                mm(O[:, i, 0:C + 1], ph, V[:, ds(t * VW, C + 1)], start=first, stop=False)
                mm(O[:, i, 0:C], ph, V[:, ds(t * VW + VL0, C)], start=False, stop=False)
                return mm(O[:, i, 0:C + 1], PL[:, slot, i * P:(i + 1) * P], V[:, ds(t * VW, C + 1)],
                          start=False, stop=last)

            def transpose_maxima(c, outputs):
                pe.wait_ge(out_ready, 2 * outputs + 2)
                pe.wait_ge(s_maxed, c * T + T)
                for i in range(MT):
                    m = nc.tensor.transpose(ST[:, 0, i * P:(i + 1) * P], MX[:, i * P:(i + 1) * P], ident[:, :])
                m.then_inc(maxt_ready, 1)

            def spread_maxima(c):
                pe.wait_ge(diag_ready, c + 1)
                mm(ST[:, 1, :], ones[:, :], diag[:, :, :].rearrange("p i n -> p (i n)"),
                   start=True, stop=True).then_inc(mb_psum, 1)

            def group(j, c, g, half, ahead, first=False):
                for k in range(GRP):
                    t = GRP * g + k
                    for n, (s, bank) in enumerate(ahead[k]):
                        if n == 0:
                            scores(j + 1, c + 1, s, bank)
                    pe.wait_ge(pl_ready, c * T + t + 1)
                    for i in range(MT):
                        if not (first and k == 0 and i == 0):
                            w = weigh(t, half * GRP + k, i, first=first and k == 0)
                        if i == 1:
                            for s, bank in ahead[k][1:]:
                                scores(j + 1, c + 1, s, bank)
                    w.then_inc(weighed, 1)

            def first_weights(c):
                pe.wait_ge(pl_ready, c * T + 1)
                weigh(0, 0, 0, first=True)

            def chunk(b, j, more):
                c = b * NCH + j
                none = [[]] * GRP
                group(j, c, 0, 0, [[(k, k % 2)] for k in range(GRP)] if more else none, first=True)
                group(j, c, 1, 1, [[(GRP + 2 * k, 0), (GRP + 2 * k + 1, 1)] for k in range(GRP)] if more else none)
                with pe.Fori(1, T // RING - 1) as p:
                    for half in range(2):
                        g = 2 * p + half
                        group(j, c, g, half, [[(GRP * g + GRP + k, k % 2)] for k in range(GRP)] if more else none)
                for k in range(GRP):
                    t = T - RING + k
                    if more and k < 3:
                        scores(j + 1, c + 1, T - GRP + (0, 1, 3)[k], (0, 1, 1)[k])
                    pe.wait_ge(pl_ready, c * T + t + 1)
                    for i in range(MT):
                        w = weigh(t, k, i)
                        if more and k == 3 and i == 1:
                            transpose_maxima(c + 1, c)
                        if more and k == 1 and i == 1:
                            scores(j + 1, c + 1, T - GRP + 2, 0)
                    w.then_inc(weighed, 1)
                for i in range(MT):
                    for k in range(GRP):
                        t = T - GRP + k
                        if i == 0:
                            pe.wait_ge(pl_ready, c * T + t + 1)
                        w = weigh(t, GRP + k, i, last=k == GRP - 1)
                        if i == MT - 1 and k < GRP - 1:
                            w.then_inc(weighed, 1)
                    w.then_inc(o_ready, 1)
                    if more and i == 0:
                        spread_maxima(c + 1)
                if more:
                    pe.wait_ge(mb_ready, c + 2)
                else:
                    pe.wait_ge(out_ready, 2 * c + 2)
                for i in range(MT):
                    if more and i == MT - 1:
                        first_weights(c + 1)
                    pe.wait_ge(osb_ready, c * MT + i + 1)
                    for h in range(H):
                        m = nc.tensor.transpose(ST[:, h, i * P:(i + 1) * P], OSB[:, i, h * P:(h + 1) * P],
                                                ident[:, :])
                        if (i, h) == (0, 0):
                            m.then_inc(weighed, 1)
                m.then_inc(ot_ready, 1)

            pe.wait_ge(consts, 4)
            pe.wait_ge(w_split, 2)
            with pe.Fori(0, BATCH) as b:
                with pe.Fori(0, NCH // MT) as r:
                    for k in range(MT):
                        i = MT * r + k
                        n = ds(i * CH, CH)
                        for h in range(H):
                            pe.wait_ge(xl_ready[h], b * NPC + 2 * r + k // 2 + 1)
                        pe.wait_ge(proj_bank_free, b * PROJ + i + 1)
                        for h in range(H):
                            mm(O[:, k, :], wqkh[:, h, :], XH[:, h, n], start=h == 0, stop=False)
                            mm(O[:, k, :], wqkl[:, h, :], XH[:, h, n], start=False, stop=False)
                            m = mm(O[:, k, :], wqkh[:, h, :], XL[:, h, n], start=False, stop=h == H - 1)
                        m.then_inc(proj_ready, 1)
                def values(i, k, lag):
                    pe.wait_ge(proj_bank_free, b * PROJ + NCH + i + MT - lag + 1)
                    for h in range(H):
                        xh, xl = XH[:, h, ds(i * P, P)], XL[:, h, ds(i * P, P)]
                        mm(O[:, k, 0:C], xh, wvh[:, h, :], start=h == 0, stop=False)
                        mm(O[:, k, 0:C], xh, wvl[:, h, :], start=False, stop=False)
                        m = mm(O[:, k, 0:C], xl, wvh[:, h, :], start=False, stop=h == H - 1)
                    m.then_inc(proj_ready, 1)

                for half in range(2):
                    with pe.Fori(half * NCH // 2, (half + 1) * NCH // 2) as r:
                        for k in range(MT):
                            if k < VR:
                                values(VR * r + k, k, VR)
                            if k == 0:
                                pe.wait_ge(fg_moved[half], 48 * (b + 1))
                            scores(0, b * NCH, MT * r + k, k % 2)
                for i in range(4):
                    values(VR * NCH + i, i, VR if i < VR else MT)
                transpose_maxima(b * NCH, b * NCH)
                values(VR * NCH + 4, 0, MT)
                values(VR * NCH + 5, 1, MT)
                spread_maxima(b * NCH)
                values(VR * NCH + 6, 2, MT)
                values(VR * NCH + 7, 3, MT)
                pe.wait_ge(proj_bank_free, (b + 1) * PROJ + MT)
                first_weights(b * NCH)
                with pe.Fori(0, NCH - 1) as j:
                    chunk(b, j, True)
                chunk(b, NCH - 1, False)

        @block.scalar
        def _(act):
            def exps(c, t, slot):
                act.wait_ge(weighed, c * T + t + 1)
                tile = SC[:, ds(t * CH, CH)]
                nc.scalar.activation(PH[:, slot, :], tile, ACT.Exp, bias=SHIFT)
                nc.scalar.activation(tile, tile, ACT.Exp, bias=SHIFT).then_inc(exp_done, 1)

            def store(c, t, bank, used=True):
                if used:
                    act.wait_ge(pl_ready, (c - 1) * T + t + 1)
                act.wait_ge(s_ready, c * T + t + 1)
                act.sem_inc(store_turn, 1)
                nc.scalar.activation(SC[:, ds(t * CH, CH)], S[:, bank, :], ACT.Copy).then_inc(s_stored, 1)

            def later_exps(c, t, slot):
                act.wait_ge(sub_ready, (T - DSUB) * c + t - DSUB + 2)
                exps(c, t, slot)

            def copy_maxima(c):
                act.wait_ge(sub_ready, (T - DSUB) * c + 1)
                act.wait_ge(mb_psum, c + 1)
                nc.scalar.copy(MB[:, :], ST[:, 1, :]).then_inc(mb_ready, 1)

            def first_exps(c, t):
                if t < DSUB:
                    act.wait_ge(sub_first, DSUB * c + t + 1)
                    exps(c, t, t)
                else:
                    later_exps(c, t, t)

            def chunk(b, j, more, norm):
                c = b * NCH + j
                for k in range(GRP):
                    later_exps(c, GRP + k, GRP + k)
                    if more:
                        store(c + 1, k, k % 2)
                for k in range(GRP):
                    later_exps(c, RING + k, k)
                    if more:
                        store(c + 1, GRP + 2 * k, 0)
                    if k == GRP - 1:
                        later_exps(c, RING + GRP, GRP)
                    if more:
                        store(c + 1, GRP + 2 * k + 1, 1)
                with act.Fori(1, T // RING - 1) as p:
                    for k in range(RING):
                        later_exps(c, RING * p + GRP + 1 + k, (GRP + 1 + k) % RING)
                        if more:
                            store(c + 1, RING * p + GRP + k, k % 2)
                for k in range(GRP):
                    if k < GRP - 1:
                        later_exps(c, T - GRP + 1 + k, GRP + 1 + k)
                    if more:
                        store(c + 1, T - GRP + k, k % 2)
                act.wait_ge(res_coefs, b + 1)
                act.wait_ge(res_in, 16 * (c + 1))
                act.wait_ge(out_stored, 16 * c + 1)
                for h in range(H):
                    nc.scalar.activation(RES[:, h, :], xin_res[:, h, :], ACT.Identity,
                                         scale=rscale[:, h:h + 1], bias=rbias[:, h:h + 1]).then_inc(res_ready, 1)
                if more:
                    copy_maxima(c + 1)
                for k in range(GRP):
                    if norm and k >= 2:
                        if k == 2:
                            act.wait_ge(xn_ready, b * NPC + j - NPC + 2)
                        nc.scalar.copy(XH[:, k - 2, ds((j - NPC) * PC, PC)], xin[:, k - 2, :]).then_inc(xh_ready, 1)
                    if more:
                        first_exps(c + 1, k)

            act.wait_ge(w_in, 64)
            nc.scalar.copy(wqkh[:, :, :], wqk[:, :, :])
            nc.scalar.copy(wvh[:, :, :], wv[:, :, :]).then_inc(w_hi, 1)
            for q in range(NPC):
                act.wait_ge(x0_normal, q + 1)
                for h in range(H):
                    nc.scalar.copy(XH[:, h, q * PC:(q + 1) * PC], x0[:, h, q * PC:(q + 1) * PC]).then_inc(xh_ready, 1)
            with act.Fori(0, BATCH) as b:
                def round_values(i, k):
                    act.wait_ge(proj_ready, b * PROJ + NCH + i + 1)
                    nc.scalar.copy(V[:, ds(i * VW, C)], O[:, k, 0:C]).then_inc(proj_hi, 1)

                with act.Fori(0, NCH // MT) as r:
                    for k in range(MT):
                        i = MT * r + k
                        n = ds(i * CH, CH)
                        act.wait_ge(proj_ready, b * PROJ + i + 1)
                        nc.scalar.copy(F1[0:CQ, n], O[0:CQ, k, :])
                        nc.scalar.copy(G1[CQ:P, n], O[CQ:P, k, :]).then_inc(proj_hi, 1)
                with act.Fori(0, NCH) as r:
                    for k in range(MT):
                        if k < VR:
                            round_values(VR * r + k, k)
                        store(b * NCH, MT * r + k, k % 2, used=False)
                for i in range(4):
                    round_values(VR * NCH + i, i)
                round_values(VR * NCH + 4, 0)
                round_values(VR * NCH + 5, 1)
                copy_maxima(b * NCH)
                round_values(VR * NCH + 6, 2)
                first_exps(b * NCH, 0)
                round_values(VR * NCH + 7, 3)
                for k in range(1, GRP):
                    first_exps(b * NCH, k)
                with act.Fori(0, NPC) as j:
                    chunk(b, j, True, False)
                with act.Fori(NPC, NCH - 1) as j:
                    chunk(b, j, True, True)
                chunk(b, NCH - 1, False, True)

        @block.vector
        def _(dve):
            ve = nc.vector

            def stepper(n, before):
                done = [before]

                def step(ins):
                    done[0] += 1
                    ins.then_inc(coef_step, 1)
                    dve.wait_ge(coef_step, n * COEF + done[0])
                return step, done

            def group_variances(n):
                step, done = stepper(n, 0)
                for h in range(H):
                    last = ve.bn_aggr(mv[:, h, :], stats[:, h, :, :].rearrange("p a b -> p (a b)"))
                step(last)
                ve.tensor_copy(cm[:, 0:H], mv[:, :, 0])
                step(ve.tensor_copy(cv[:, 0:H], mv[:, :, 1]))
                flat = "p a b -> p (a b)"
                ve.transpose(tm[:, :, :].rearrange(flat), cm[:, :])
                step(ve.transpose(tv[:, :, :].rearrange(flat), cv[:, :]))
                step(ve.tensor_reduce(gmean[:, :], tm[:, :, :], axis=AX.X, op=ALU.add))
                step(ve.tensor_scalar(gmean[:, :], gmean[:, :], 1.0 / GN, None, ALU.mult))
                spread = gmean[:, :].unsqueeze(2).to_broadcast([P, NG, GN])
                ve.tensor_copy(bm[:, :, :], spread)
                step(ve.tensor_tensor(tm[:, :, :], tm[:, :, :], spread, ALU.subtract))
                step(ve.tensor_tensor(tm[:, :, :], tm[:, :, :], tm[:, :, :], ALU.mult))
                step(ve.tensor_tensor(tv[:, :, :], tv[:, :, :], tm[:, :, :], ALU.add))
                step(ve.tensor_reduce(gvar[:, :], tv[:, :, :], axis=AX.X, op=ALU.add))
                step(ve.tensor_scalar(gvar[:, :], gvar[:, :], 1.0 / GN, EPS, ALU.mult, ALU.add))
                assert done[0] == COEF_VAR

            def inverse_roots(n):
                step, done = stepper(n, COEF_VAR)
                flat = "p a b -> p (a b)"
                step(ve.tensor_scalar(gt[:, :].bitcast(i32), gvar[:, :].bitcast(i32), 1, None,
                                      ALU.logical_shift_right))
                step(ve.tensor_scalar(gr[:, :].bitcast(i32), gt[:, :].bitcast(i32), -1.0, float(RSQRT_GUESS),
                                      ALU.mult, ALU.add))
                for _ in range(3):
                    step(ve.scalar_tensor_tensor(gt[:, :], gr[:, :], -0.5, gr[:, :], ALU.mult, ALU.mult))
                    step(ve.tensor_tensor(gt[:, :], gt[:, :], gvar[:, :], ALU.mult))
                    step(ve.scalar_tensor_tensor(gr[:, :], gt[:, :], 1.5, gr[:, :], ALU.add, ALU.mult))
                ve.transpose(nmean[:, :], bm[:, :, :].rearrange(flat))
                step(ve.tensor_copy(br[:, :, :], gr[:, :].unsqueeze(2).to_broadcast([P, NG, GN])))
                assert done[0] == COEF
                ve.transpose(nrstd[:, :], br[:, :, :].rearrange(flat)).then_inc(coefs_ready, 1)

            def normalise(dst, src, h):
                return ve.tensor_scalar(dst, src, nmean[:, h:h + 1], nrstd[:, h:h + 1], ALU.subtract, ALU.mult)

            def maximum(c, t, first=False):
                dve.wait_ge(s_stored, c * T + t + 3)
                tile = SC[:, ds(t * CH, CH)]
                if first:
                    ve.tensor_copy(MX[:, :], tile).then_inc(s_maxed, 1)
                else:
                    dve.wait_ge(s_maxed, c * T + t)
                    ve.tensor_tensor(MX[:, :], tile, MX[:, :], ALU.max).then_inc(s_maxed, 1)

            def max_diagonals(c):
                dve.wait_ge(maxt_ready, c + 1)
                ve.tensor_reduce(mxc[:, :], ST[:, 0, :].rearrange("p (i n) -> p i n", n=P), axis=AX.X,
                                 op=ALU.max).then_inc(mxc_ready, 1)
                dve.wait_ge(mxc_ready, c + 1)
                ve.tensor_tensor(diag[:, :, :], ident[:, :].unsqueeze(1).to_broadcast([P, MT, P]),
                                 mxc[:, :].unsqueeze(2).to_broadcast([P, MT, P]),
                                 ALU.mult).then_inc(diag_ready, 1)

            def subtract_first(c):
                dve.wait_ge(mb_ready, c + 1)
                for t in range(DSUB):
                    tile = SC[:, t * CH:(t + 1) * CH]
                    ve.tensor_tensor(tile, tile, MB[:, :], ALU.subtract).then_inc(sub_first, 1)

            def low_part(c, t, slot):
                dve.wait_ge(exp_done, c * T + t + 1)
                ve.tensor_tensor(PL[:, slot, :], SC[:, ds(t * CH, CH)], PH[:, slot, :],
                                 ALU.subtract).then_inc(pl_ready, 1)

            def piece_statistics(j, a):
                for h in range(H):
                    last = ve.bn_stats(stats[:, h, ds(2 * j + a, 1), :], xin[:, h, a * CH:(a + 1) * CH])
                return last

            def chunk(b, j, more, norm, coefs=False):
                c = b * NCH + j
                for k in range(GRP):
                    low_part(c, GRP + k, GRP + k)
                    if more:
                        maximum(c + 1, k, first=k == 0)
                if coefs:
                    group_variances(b + 1)
                for k in range(GRP):
                    low_part(c, RING + k, k)
                    if more:
                        maximum(c + 1, GRP + 2 * k)
                    if k == GRP - 1:
                        low_part(c, RING + GRP, GRP)
                    if more:
                        maximum(c + 1, GRP + 2 * k + 1)
                with dve.Fori(1, T // RING - 1) as p:
                    for k in range(RING):
                        low_part(c, RING * p + GRP + 1 + k, (GRP + 1 + k) % RING)
                        if more:
                            maximum(c + 1, RING * p + GRP + k)
                if not norm:
                    dve.wait_ge(xin_in, 16 * (c + 1))
                    piece_statistics(j, 0)
                for k in range(GRP):
                    if k < GRP - 1:
                        low_part(c, T - GRP + 1 + k, GRP + 1 + k)
                    if more:
                        maximum(c + 1, T - GRP + k)
                if more:
                    max_diagonals(c + 1)
                if norm:
                    if coefs:
                        inverse_roots(b + 1)
                    dve.wait_ge(coefs_ready, b + 2)
                    dve.wait_ge(xin_in, 16 * (c + 1))
                    for h in range(H):
                        last = normalise(xin[:, h, :], xin[:, h, :], h)
                    last.then_inc(xn_ready, 1)
                else:
                    piece_statistics(j, 1).then_inc(xin_read, 1)
                for i in range(MT):
                    dve.wait_ge(o_ready, c * MT + i + 1)
                    ve.reciprocal(rden[:, i:i + 1], O[:, i, C:C + 1]).then_inc(rden_ready, 1)
                    dve.wait_ge(rden_ready, c * MT + i + 1)
                    ve.tensor_scalar(OSB[:, i, :], O[:, i, 0:C], rden[:, i:i + 1], gam[:, :],
                                     ALU.mult, ALU.mult).then_inc(osb_ready, 1)
                    if more and i == 0:
                        subtract_first(c + 1)
                    if more and 0 < i < MT - 1:
                        low_part(c + 1, i - 1, i - 1)
                if more:
                    low_part(c + 1, MT - 2, MT - 2)
                dve.wait_ge(res_ready, 2 * c + 3)
                dve.wait_ge(ot_ready, c + 1)
                for h in range(H):
                    ve.tensor_tensor(RES[:, h, :], ST[:, h, :], RES[:, h, :], ALU.add).then_inc(out_ready, 1)
                if more:
                    low_part(c + 1, MT - 1, MT - 1)

            ve.memset(cm[:, :], 0.0).then_inc(s_stored, 2)
            ve.memset(cv[:, :], 1.0)
            ve.memset(mxc[:, 0:1], 0.0).then_inc(proj_bank_free, MT)
            ve.memset(mxc[:, 1:2], 0.0).then_inc(weighed, RING)
            ve.memset(mxc[:, 2:3], 0.0).then_inc(sub_ready, 1)
            ve.memset(gmean[:, :], 0.0).then_inc(xn_ready, 1)
            for k, credited in enumerate((xin_read, res_ready, out_stored)):
                ve.memset(rden[:, k:k + 1], 0.0).then_inc(credited, 1)
            ve.memset(rden[:, 3:4], 0.0).then_inc(out_ready, 2)
            for q in range(NPC):
                dve.wait_ge(x0_in[q], 16)
                for a in range(q * PC // CH, (q + 1) * PC // CH):
                    for h in range(H):
                        last = ve.bn_stats(stats[:, h, a, :], x0[:, h, a * CH:(a + 1) * CH])
            last.then_inc(xin_read, 1)
            dve.wait_ge(xin_read, 2)
            group_variances(0)
            inverse_roots(0)
            dve.wait_ge(coefs_ready, 1)
            for q in range(NPC + 1):
                if q < NPC:
                    for h in range(H):
                        last = normalise(x0[:, h, q * PC:(q + 1) * PC], x0[:, h, q * PC:(q + 1) * PC], h)
                    last.then_inc(x0_normal, 1)
                if q > 0:
                    dve.wait_ge(xh_ready, 2 * q)
                    cols = slice((q - 1) * PC, q * PC)
                    ve.tensor_tensor(XL[:, 0, cols], x0[:, 0, cols], XH[:, 0, cols],
                                     ALU.subtract).then_inc(xl_ready[0], 1)
                if q == 0:
                    dve.wait_ge(w_hi, 1)
                    ve.tensor_tensor(wqkl[:, :, :], wqk[:, :, :], wqkh[:, :, :], ALU.subtract).then_inc(w_split, 1)
                    ve.tensor_tensor(wvl[:, :, :], wv[:, :, :], wvh[:, :, :], ALU.subtract).then_inc(w_split, 1)

            with dve.Fori(0, BATCH) as b:
                def split_values(i, k):
                    dve.wait_ge(proj_hi, b * PROJ + NCH + i + 1)
                    ve.tensor_tensor(V[:, ds(i * VW + VL0, C)], O[:, k, 0:C], V[:, ds(i * VW, C)],
                                     ALU.subtract).then_inc(proj_bank_free, 1)

                with dve.Fori(0, NCH // MT) as r:
                    for k in range(MT):
                        i = MT * r + k
                        n = ds(i * CH, CH)
                        dve.wait_ge(proj_hi, b * PROJ + i + 1)
                        ve.tensor_tensor(FL[:, n], O[0:CQ, k, :], F1[0:CQ, n], ALU.subtract)
                        ve.tensor_tensor(GL[CQ:P, n], O[CQ:P, k, :], G1[CQ:P, n],
                                         ALU.subtract).then_inc(proj_bank_free, 1)
                def first_maxima(r, first):
                    for k in range(MT):
                        if k < VR:
                            split_values(VR * r + k, k)
                        maximum(b * NCH, MT * r + k, first=first and k == 0)

                first_maxima(0, True)
                with dve.Fori(1, NCH) as r:
                    first_maxima(r, False)
                split_values(VR * NCH, 0)
                split_values(VR * NCH + 1, 1)
                max_diagonals(b * NCH)
                split_values(VR * NCH + 2, 2)
                split_values(VR * NCH + 3, 3)
                split_values(VR * NCH + 4, 0)
                split_values(VR * NCH + 5, 1)
                subtract_first(b * NCH)
                split_values(VR * NCH + 6, 2)
                split_values(VR * NCH + 7, 3)
                for k in range(GRP):
                    low_part(b * NCH, k, k)
                dve.wait_ge(coefs_ready, b + 1)
                ve.tensor_scalar(rscale[:, :], nrstd[:, 0:H], 1.0, None, ALU.add)
                ve.scalar_tensor_tensor(rbias[:, :], nmean[:, 0:H], -1.0, nrstd[:, 0:H],
                                        ALU.mult, ALU.mult).then_inc(res_coefs, 1)
                with dve.Fori(0, NPC) as j:
                    chunk(b, j, True, False)
                chunk(b, NPC, True, True, coefs=True)
                with dve.Fori(NPC + 1, NCH - 1) as j:
                    chunk(b, j, True, True)
                chunk(b, NCH - 1, False, True)


def kernel(**inputs):
    import numpy as np
    import concourse.bacc as bacc
    from concourse.bass_utils import run_bass_kernel_spmd

    f32 = mybir.dt.float32
    x = np.ascontiguousarray(inputs["x"])
    b, c, hh, ww = x.shape
    arrays = {
        "x": x.reshape(b, c, hh * ww),
        "wqT": np.ascontiguousarray(np.transpose(inputs["L0_conv_Wq"])),
        "wkT": np.ascontiguousarray(np.transpose(inputs["L0_conv_Wk"])),
        "wvT": np.ascontiguousarray(np.transpose(inputs["L0_conv_Wv"])),
        "gamma": np.ascontiguousarray(np.broadcast_to(np.asarray(inputs["L0_conv_gamma"]).reshape(1, 1), (128, 1))),
    }
    nc = bacc.Bacc("TRN2", target_bir_lowering=False, num_devices=1)
    args = [nc.dram_tensor(n, a.shape, f32, kind="ExternalInput").ap() for n, a in arrays.items()]
    out = nc.dram_tensor("out", (b, c, hh * ww), f32, kind="ExternalOutput").ap()
    groupnorm_attention(nc, *args, out)
    r = run_bass_kernel_spmd(nc, [arrays], core_ids=[0])
    return r.results[0]["out"].reshape(b, c, hh, ww)
```
